# Optimizing a Trainium2 kernel written in Bass

```python
import numpy as np
import jax
import jax.numpy as jnp

def _softmax(x, axis=-1):
    return jax.nn.softmax(x, axis=axis)

def _gelu(x):
    return jax.nn.gelu(x, approximate=True)

def _silu(x):
    return jax.nn.silu(x)

def _sigmoid(x):
    return jax.nn.sigmoid(x)

def _layernorm(x, axis=-1, eps=1e-05):
    m = jnp.mean(x, axis=axis, keepdims=True)
    v = jnp.var(x, axis=axis, keepdims=True)
    return (x - m) / jnp.sqrt(v + eps)

def _scatter_add(tgt, idx, src, axis=0):
    return tgt.at[idx].add(src)

def _segment_sum(src, seg, n):
    return jax.ops.segment_sum(src, seg, n)
kernel_name = 'mk_adj_resnorm_d2_adj_r2_773fdf'

def setup_inputs(seed: int=0):
    np.random.seed(seed)
    _w = jnp.asarray

    def _rec_inputs():
        import jax
        import jax.numpy as jnp
        _gk = jax.random.key(seed)
        x = -9.229e-05 + 0.9999 * jax.random.normal(jax.random.fold_in(_gk, 1), (32, 256, 512), jnp.float32)
        _a = jax.random.bernoulli(jax.random.fold_in(_gk, 2), 0.0078125, (256, 256))
        _a = jnp.logical_or(_a, jnp.swapaxes(_a, -1, -2))
        _a = jnp.logical_or(_a, jnp.eye(256, dtype=bool))
        _af = _a.astype(jnp.float32)
        adj = _af
        return (x, adj)
    x, adj = _rec_inputs()

    def _L0_gnn_setup():
        import jax, jax.numpy as jnp
        import numpy as np
        DIM = 199
        K_HOP = 3

        def _khop_support(n, k):
            A = np.eye(n, dtype=np.float64)
            idx = np.arange(n)
            A[idx, (idx + 1) % n] = 1.0
            A[(idx + 1) % n, idx] = 1.0
            S = np.linalg.matrix_power(A, k)
            return (S > 0).astype(np.float32)
        key = jax.random.key(seed)
        kx, kk = jax.random.split(key)
        batch, n, f = (128, DIM, 512)
        x = jax.random.normal(kx, (batch, n, f), dtype=jnp.float32)
        support = jnp.asarray(_khop_support(n, K_HOP))
        limit = float(np.sqrt(6.0 / (n + n)))
        kernel = jax.random.uniform(kk, (n, n), minval=-limit, maxval=limit, dtype=jnp.float32)
        bias = jnp.zeros((f,), dtype=jnp.float32)
        return {'x': x, 'support': support, 'kernel': kernel, 'bias': bias}
    _L0_gnn_all = _L0_gnn_setup()
    _L0_gnn_in = {k: v for k, v in _L0_gnn_all.items() if k in ('bias',)}
    del _L0_gnn_all

    def _L1_gnn_setup():
        import jax, jax.numpy as jnp
        import numpy as np
        EPS = 1e-08

        def _row_stochastic_causal(A, causal_mask):
            A = A * causal_mask
            deg = jnp.maximum(A.sum(axis=-1, keepdims=True), EPS)
            return A / deg
        key = jax.random.key(seed)
        k = jax.random.split(key, 5)
        B, N, D = (4, 1024, 512)
        s = 1.0 / np.sqrt(D)
        h = jax.random.normal(k[0], (B, N, D), dtype=jnp.float32)
        W_lang = jax.random.normal(k[1], (D, D), dtype=jnp.float32) * s
        W_grav = jax.random.normal(k[2], (D, D), dtype=jnp.float32) * s
        W_V = jax.random.normal(k[3], (D, D), dtype=jnp.float32) * s
        W_O = jax.random.normal(k[4], (D, D), dtype=jnp.float32) * s
        causal_mask = jnp.tril(jnp.ones((N, N), dtype=jnp.float32))
        gate_logit = jnp.zeros((), jnp.float32)
        log_sigma = jnp.zeros((), jnp.float32)
        return {'h': h, 'causal_mask': causal_mask, 'W_lang': W_lang, 'W_grav': W_grav, 'W_V': W_V, 'W_O': W_O, 'gate_logit': gate_logit, 'log_sigma': log_sigma}
    _L1_gnn_all = _L1_gnn_setup()
    _L1_gnn_in = {k: v for k, v in _L1_gnn_all.items() if k in ('W_lang', 'W_grav', 'W_V', 'W_O', 'gate_logit', 'log_sigma')}
    del _L1_gnn_all
    return {'x': x, 'adj': adj, 'L0_gnn_bias': _L0_gnn_in['bias'], 'L1_gnn_W_lang': _L1_gnn_in['W_lang'], 'L1_gnn_W_grav': _L1_gnn_in['W_grav'], 'L1_gnn_W_V': _L1_gnn_in['W_V'], 'L1_gnn_W_O': _L1_gnn_in['W_O'], 'L1_gnn_gate_logit': _L1_gnn_in['gate_logit'], 'L1_gnn_log_sigma': _L1_gnn_in['log_sigma']}

def reference(x, adj, L0_gnn_bias, L1_gnn_W_lang, L1_gnn_W_grav, L1_gnn_W_V, L1_gnn_W_O, L1_gnn_gate_logit, L1_gnn_log_sigma):
    import jax
    import jax.numpy as jnp

    def _L0_gnn_ref(x, support, kernel, bias):
        import jax, jax.numpy as jnp
        import numpy as np
        DIM = 199
        K_HOP = 3

        def _khop_support(n, k):
            A = np.eye(n, dtype=np.float64)
            idx = np.arange(n)
            A[idx, (idx + 1) % n] = 1.0
            A[(idx + 1) % n, idx] = 1.0
            S = np.linalg.matrix_power(A, k)
            return (S > 0).astype(np.float32)
        W = support * kernel
        out = jnp.einsum('bnf,nm->bmf', x, W)
        out = out + bias
        return out

    def _L1_gnn_ref(h, causal_mask, W_lang, W_grav, W_V, W_O, gate_logit, log_sigma):
        import jax, jax.numpy as jnp
        import numpy as np
        EPS = 1e-08

        def _row_stochastic_causal(A, causal_mask):
            A = A * causal_mask
            deg = jnp.maximum(A.sum(axis=-1, keepdims=True), EPS)
            return A / deg
        z_l = jnp.einsum('bnd,ed->bne', h, W_lang)
        z_g = jnp.einsum('bnd,ed->bne', h, W_grav)
        v = jnp.einsum('bnd,ed->bne', h, W_V)
        N = h.shape[-2]
        not_eye = 1.0 - jnp.eye(N, dtype=h.dtype)
        zn = z_l / jnp.maximum(jnp.linalg.norm(z_l, axis=-1, keepdims=True), EPS)
        A_l = jnp.maximum(jnp.einsum('bnd,bmd->bnm', zn, zn), 0.0) * not_eye
        sq = jnp.sum(z_g * z_g, axis=-1, keepdims=True)
        d2 = jnp.maximum(sq + jnp.swapaxes(sq, -1, -2) - 2.0 * jnp.einsum('bnd,bmd->bnm', z_g, z_g), 0.0)
        sigma = jnp.exp(log_sigma)
        A_g = jnp.exp(-d2 / (2.0 * sigma * sigma)) * not_eye
        K_l = _row_stochastic_causal(A_l, causal_mask)
        K_g = _row_stochastic_causal(A_g, causal_mask)
        w_l = jax.nn.sigmoid(gate_logit)
        K = w_l * K_l + (1.0 - w_l) * K_g
        out = jnp.einsum('bnm,bmd->bnd', K, v)
        return jnp.einsum('bnd,ed->bne', out, W_O)
    x = _layernorm(x + _L0_gnn_ref(x, adj, adj, L0_gnn_bias), axis=-1)
    x = _layernorm(x + _L1_gnn_ref(x, adj, L1_gnn_W_lang, L1_gnn_W_grav, L1_gnn_W_V, L1_gnn_W_O, L1_gnn_gate_logit, L1_gnn_log_sigma), axis=-1)
    return x

_drawn_inputs = setup_inputs


def setup_inputs(seed=0):
    import zlib

    import numpy as np

    out = dict(_drawn_inputs(seed))
    spreads = {'L0_gnn_bias': (0.0, 0.1)}
    factors = {}
    for name, (base, spread) in spreads.items():
        noise = np.random.default_rng([zlib.crc32(name.encode()), seed]).standard_normal(out[name].shape)
        drawn = base * np.exp(spread * noise) if base else spread * noise
        out[name] = jnp.asarray(drawn.astype(out[name].dtype))
    for name, factor in factors.items():
        out[name] = (out[name] * factor).astype(out[name].dtype)
    return out
```

```python
from contextlib import ExitStack

import concourse.bass as bass
from concourse import mybir

F32 = mybir.dt.float32
F32R = mybir.dt.float32r
ALU = mybir.AluOpType
ACT = mybir.ActivationFunctionType
AX_X = mybir.AxisListType.X

P = 128
LN_EPS = 1e-5
EPS = 1e-8

PRODUCTS = ((0, 0), (0, 1), (1, 0))


def bass_adj_resnorm_kernel(nc, x, adj, bias, w_lang_t, w_grav_t, w_v, w_o_t, gate, log_sigma, out):
    B, N, D = x.shape
    PAIR = 2
    J = N // P
    T = PAIR * J
    C = D // P
    TOK = PAIR * N
    G = B // PAIR
    assert N == 2 * P and D == 512 and TOK == 512 and T == 4 and C == 4 and G >= 5

    x_pairs = x.rearrange("b n f -> (b n) f").rearrange("(g t p) f -> g p t f", t=T, p=P)
    out_pairs = out.rearrange("b n f -> (b n) f").rearrange("(g t p) f -> g p t f", t=T, p=P)

    with ExitStack() as ctx:
        def sb(name, shape, dt=F32):
            return ctx.enter_context(nc.sbuf_tensor(name, shape, dt))

        def sem(name):
            return ctx.enter_context(nc.semaphore(name))

        def split(name, shape):
            return [sb(name + "_hi", shape, F32R), sb(name + "_lo", shape, F32R)]

        x_raw = sb("x_raw", [P, T, D])
        x_s = split("x", [P, T, D])
        mixed = sb("mixed", [P, T, D])
        h_new = sb("h_new", [P, T, D])
        h_res = sb("h_res", [P, T, D])
        h_t = split("h_t", [P, C, TOK])
        zl_t = split("zl_t", [P, C, TOK])
        zg_t = split("zg_t", [P, C, TOK])
        v_s = split("v", [P, T, D])
        y = sb("y", [P, T, D])
        wl_s = split("wl", [P, C, D])
        wg_s = split("wg", [P, C, D])
        wvo_s = split("wvo", [P, C, D])
        mix_s = split("mix", [P, J, N])
        mix_w = sb("mix_w", [P, J, N])
        mask = sb("mask", [P, J, N])
        bias_b = sb("bias_b", [P, D])
        ident = sb("ident", [P, J, P])
        aff = sb("aff", [P, 2, T, N])
        a_l, a_g = aff[:, 0], aff[:, 1]
        k_nm = sb("k_nm", [P, T, N])
        k_t = split("k_t", [P, T, N])
        row_r = sb("row_r", [P, T * P])
        row_sq = sb("row_sq", [P, T * P])
        diag = sb("diag", [P, 2 * PAIR, J, P])
        norm2 = sb("norm2", [P, 2, T])
        guarded = sb("guarded", [P, T])
        r_l = sb("r_l", [P, T])
        deg = sb("deg", [P, 2, T])
        deg_max = sb("deg_max", [P, 2, T])
        deg_inv = sb("deg_inv", [P, 2, T])
        coef = sb("coef", [P, 2, T])
        branch_w = sb("branch_w", [P, 2, T])
        stats1 = sb("stats1", [P, T, 6])
        mv1 = sb("mv1", [P, T, 2])
        rstd1 = sb("rstd1", [P, 4, T])
        stats2 = sb("stats2", [P, T, 6])
        mv2 = sb("mv2", [P, T, 2])
        rstd2 = sb("rstd2", [P, 4, T])
        minus_half = sb("minus_half", [P, T])
        scal = sb("scal", [P, 8])
        d2_scale = scal[:, 7:8]

        bank = [ctx.enter_context(nc.psum_tensor(f"bank{i}", [P, 512], F32)) for i in range(8)]

        wl_raw, wg_raw, wv_raw = mixed[:], h_res[:], y[:]
        wo_raw = aff[:].rearrange("p a t n -> p (a t n)").rearrange("p (c e) -> p c e", c=C)

        ZL, ZG, GRAM_L, KT, GRAM_G = (0, 1, 2, 3), (4, 5, 6, 7), (0, 1), (2, 3), (4, 5)
        AGG, VAL, ROWS, HT, MIX = (6, 7, 2, 3), (6, 7, 2, 3), (0, 1), (4, 5, 6, 7), (0, 1, 2, 3)

        consts_loaded = sem("consts_loaded")
        wl_loaded = sem("wl_loaded")
        wg_loaded = sem("wg_loaded")
        vo_loaded = sem("vo_loaded")
        ident_made = sem("ident_made")
        gates_exp = sem("gates_exp")
        gates_step = sem("gates_step")
        mix_made = sem("mix_made")
        weights_hi = sem("weights_hi")
        weights_split = sem("weights_split")
        wvo_ready = sem("wvo_ready")
        wvo_hi = sem("wvo_hi")
        wvo_split = sem("wvo_split")
        mask_made = sem("mask_made")

        x_loaded = sem("x_loaded")
        x_hi_made = sem("x_hi_made")
        x_split = sem("x_split")
        mix_ready = sem("mix_ready")
        mix_out = sem("mix_out")
        stats1_made = sem("stats1_made")
        mean1_made = sem("mean1_made")
        rstd1_step = sem("rstd1_step")
        h_ready = sem("h_ready")
        h_saved = sem("h_saved")
        ht_ready = sem("ht_ready")
        ht_hi = sem("ht_hi")
        ht_split = sem("ht_split")
        zl_ready = sem("zl_ready")
        zl_hi = sem("zl_hi")
        zl_split = sem("zl_split")
        zg_ready = sem("zg_ready")
        zg_hi = sem("zg_hi")
        zg_split = sem("zg_split")
        gram_l_ready = sem("gram_l_ready")
        gram_g_ready = sem("gram_g_ready")
        diag_cut = sem("diag_cut")
        diag_l = sem("diag_l")
        diag_g = sem("diag_g")
        r_guarded = sem("r_guarded")
        r_made = sem("r_made")
        al_out = sem("al_out")
        ag_out = sem("ag_out")
        rows_ready = sem("rows_ready")
        rows_out = sem("rows_out")
        al_masked = sem("al_masked")
        d2_made = sem("d2_made")
        exp_made = sem("exp_made")
        al_made = sem("al_made")
        ag_made = sem("ag_made")
        coef_step = sem("coef_step")
        al_scaled = sem("al_scaled")
        k_made = sem("k_made")
        kt_ready = sem("kt_ready")
        kt_hi = sem("kt_hi")
        kt_split = sem("kt_split")
        v_ready = sem("v_ready")
        v_hi = sem("v_hi")
        v_split = sem("v_split")
        agg_ready = sem("agg_ready")
        y_sum = sem("y_sum")
        stats2_made = sem("stats2_made")
        mean2_made = sem("mean2_made")
        rstd2_step = sem("rstd2_step")
        y_ready = sem("y_ready")
        stored = sem("stored")

        def later(i):
            return not (isinstance(i, int) and i <= 0)

        block = ctx.enter_context(nc.Block())

        @block.sync
        def _(sp):
            def load_x(k):
                if later(k):
                    sp.wait_ge(x_split, k)
                sp.dma_start(x_raw[:], x_pairs[bass.ds(k, 1)].rearrange("g p t f -> p (g t) f")).then_inc(x_loaded, 16)

            def store(k):
                sp.wait_ge(y_ready, k * T + T)
                sp.dma_start(out_pairs[bass.ds(k, 1)].rearrange("g p t f -> p (g t) f"), y[:]).then_inc(stored, 16)

            load_x(0)
            sp.dma_start(mask[:], adj.rearrange("(j p) m -> p j m", p=P)).then_inc(consts_loaded, 16)
            sp.dma_start(bias_b[:], bias.broadcast_to([P, D])).then_inc(consts_loaded, 16)
            sp.dma_start(scal[:, 0:1], gate.broadcast_to([P, 1])).then_inc(consts_loaded, 16)
            sp.dma_start(scal[:, 1:2], log_sigma.broadcast_to([P, 1])).then_inc(consts_loaded, 16)
            sp.dma_start(wl_raw, w_lang_t.rearrange("(c p) e -> p c e", p=P)).then_inc(wl_loaded, 16)
            sp.dma_start(wg_raw, w_grav_t.rearrange("(c p) e -> p c e", p=P)).then_inc(wg_loaded, 16)
            sp.dma_start(wv_raw, w_v.rearrange("(c p) e -> p c e", p=P)).then_inc(vo_loaded, 16)
            sp.dma_start(wo_raw, w_o_t.rearrange("(c p) e -> p c e", p=P)).then_inc(vo_loaded, 16)
            load_x(1)
            load_x(2)
            load_x(3)
            with sp.Fori(1, G - 3) as i:
                store(i - 1)
                load_x(i + 3)
            for k in range(G - 4, G):
                store(k)
            sp.wait_ge(stored, 16 * G)


        @block.gpsimd
        def _(pool):
            def split_x(k):
                pool.wait_ge(x_loaded, k * 16 + 16)
                if later(k):
                    pool.wait_ge(mix_ready, k * T)
                pool.nop(nofuse=True)
                nc.gpsimd.tensor_copy(x_s[0][:], x_raw[:]).then_inc(x_hi_made, 1)
                pool.wait_ge(x_hi_made, k + 1)
                nc.gpsimd.tensor_tensor(x_s[1][:], x_raw[:], x_s[0][:].bitcast(F32), ALU.subtract).then_inc(x_split, 1)

            def norm_factors(k, mv, f, mean_made, step):
                pool.wait_ge(mean_made, k * T + T)
                pool.nop(nofuse=True)
                nc.gpsimd.tensor_scalar(f[:, 0, :], mv[:, :, 1], LN_EPS, None, ALU.add).then_inc(step, 1)
                nc.gpsimd.tensor_scalar(f[:, 1, :], mv[:, :, 0], -1.0, None, ALU.mult).then_inc(step, 1)
                pool.wait_ge(step, k * 4 + 1)
                nc.gpsimd.tensor_tensor(f[:, 2, :], f[:, 0, :], minus_half[:], ALU.pow).then_inc(step, 1)
                pool.wait_ge(step, k * 4 + 3)
                nc.gpsimd.tensor_tensor(f[:, 3, :], f[:, 1, :], f[:, 2, :], ALU.mult).then_inc(step, 1)

            def lang_norms(i):
                pool.wait_ge(diag_l, i * PAIR + PAIR)
                pool.nop(nofuse=True)
                nc.gpsimd.tensor_scalar(guarded[:], norm2[:, 0, :], EPS * EPS, None, ALU.max).then_inc(r_guarded, 1)
                pool.wait_ge(r_guarded, i + 1)
                if later(i):
                    pool.wait_ge(rows_ready, i * 2)
                nc.gpsimd.tensor_tensor(r_l[:], guarded[:], minus_half[:], ALU.pow).then_inc(r_made, 1)

            def save_h(i):
                if later(i):
                    pool.wait_ge(y_sum, i * T)
                else:
                    pool.wait_ge(weights_split, 2)
                pool.nop(nofuse=True)
                nc.gpsimd.tensor_copy(h_res[:], h_new[:]).then_inc(h_saved, 1)

            def affinity_parts(i):
                for b in range(PAIR):
                    pool.wait_ge(al_out, i * T + J * b + J)
                    if not later(i) and b == 0:
                        pool.wait_ge(mask_made, 1)
                    nc.gpsimd.tensor_tensor(a_l[:, J * b:J * b + J], a_l[:, J * b:J * b + J], mask[:],
                                            ALU.mult).then_inc(al_masked, 1)
                pool.wait_ge(rows_out, i * 2 + 2)
                for b in range(PAIR):
                    pool.wait_ge(ag_out, i * T + J * b + J)
                    for j in range(J):
                        t = J * b + j
                        last = nc.gpsimd.tensor_tensor(a_g[:, t], a_g[:, t], row_sq[:, N * b:N * b + N], ALU.add)
                    last.then_inc(d2_made, 1)

            def body(i, mix_ahead, norm_ahead):
                if norm_ahead:
                    norm_factors(i + 1, mv1, rstd1, mean1_made, rstd1_step)
                if mix_ahead:
                    split_x(i + 2)
                lang_norms(i)
                save_h(i)
                if later(i):
                    norm_factors(i - 1, mv2, rstd2, mean2_made, rstd2_step)
                affinity_parts(i)

            nc.gpsimd.memset(minus_half[:], -0.5)
            nc.gpsimd.memset(branch_w[:], 1.0)
            nc.gpsimd.memset(ident[:], 0.0).then_inc(ident_made, 1)
            pool.wait_ge(ident_made, 1)
            nc.gpsimd.affine_select(out=ident[:], in_=ident[:], compare_op=ALU.not_equal, fill=1.0, base=0,
                                    pattern=[[0, J], [-1, P]], channel_multiplier=1).then_inc(ident_made, 1)
            split_x(0)
            pool.wait_ge(mix_made, 1)
            nc.gpsimd.affine_select(out=mask[:], in_=mask[:], compare_op=ALU.not_equal, fill=0.0, base=0,
                                    pattern=[[P, J], [-1, N]], channel_multiplier=1).then_inc(mask_made, 1)
            norm_factors(0, mv1, rstd1, mean1_made, rstd1_step)
            split_x(1)
            body(0, True, True)
            body(1, True, True)
            with pool.Fori(2, G - 2) as i:
                body(i, True, True)
            body(G - 2, False, True)
            body(G - 1, False, False)
            norm_factors(G - 1, mv2, rstd2, mean2_made, rstd2_step)

        @block.scalar
        def _(act):
            def hi(dst, src):
                return nc.scalar.activation(dst, src, ACT.Identity)

            def norm1(k):
                act.wait_ge(rstd1_step, k * 4 + 4)
                if later(k):
                    act.wait_ge(h_saved, k)
                    act.wait_ge(ht_ready, k * C)
                for t in range(T):
                    nc.scalar.activation(h_new[:, t], mixed[:, t], ACT.Identity, bias=rstd1[:, 3, t:t + 1],
                                         scale=rstd1[:, 2, t:t + 1]).then_inc(h_ready, 1)

            def norm2_out(k):
                act.wait_ge(rstd2_step, k * 4 + 4)
                for t in range(T):
                    nc.scalar.activation(y[:, t], y[:, t], ACT.Identity, bias=rstd2[:, 3, t:t + 1],
                                         scale=rstd2[:, 2, t:t + 1]).then_inc(y_ready, 1)

            def ht_his(k):
                if later(k):
                    act.wait_ge(v_ready, k * T)
                for c in range(C):
                    act.wait_ge(ht_ready, k * C + c + 1)
                    hi(h_t[0][:, c], bank[HT[c]][:]).then_inc(ht_hi, 1)

            def val_his(i, ts):
                if later(i):
                    act.wait_ge(agg_ready, i * T)
                for t in ts:
                    act.wait_ge(v_ready, i * T + t + 1)
                    hi(v_s[0][:, t], bank[VAL[t]][:]).then_inc(v_hi, 1)

            def exps(i):
                for b in range(PAIR):
                    act.wait_ge(d2_made, i * PAIR + b + 1)
                    nc.scalar.activation(a_g[:, J * b:J * b + J], a_g[:, J * b:J * b + J], ACT.Exp,
                                         scale=d2_scale).then_inc(exp_made, 1)

            def scale_lang(i):
                act.wait_ge(coef_step, i * 3 + 3)
                for t in range(T):
                    nc.scalar.activation(a_l[:, t], a_l[:, t], ACT.Identity,
                                         scale=coef[:, 0, t:t + 1]).then_inc(al_scaled, 1)

            def kt_his(i):
                if later(i - 1):
                    act.wait_ge(agg_ready, i * T)
                for b in range(PAIR):
                    act.wait_ge(kt_ready, i * PAIR + b + 1)
                    hi(k_t[0][:, J * b:J * b + J], bank[KT[b]][:]).then_inc(kt_hi, 1)

            def body(i, norm_ahead):
                prev = later(i)
                if prev:
                    act.wait_ge(gram_l_ready, i * PAIR)
                for e in range(C):
                    act.wait_ge(zl_ready, i * C + e + 1)
                    hi(zl_t[0][:, e], bank[ZL[e]][:]).then_inc(zl_hi, 1)
                    if prev and e == 0:
                        exps(i - 1)
                if prev:
                    act.wait_ge(gram_g_ready, i * PAIR)
                for e in range(C):
                    act.wait_ge(zg_ready, i * C + e + 1)
                    hi(zg_t[0][:, e], bank[ZG[e]][:]).then_inc(zg_hi, 1)
                    if prev and e == 1:
                        scale_lang(i - 1)
                if prev:
                    kt_his(i - 1)
                act.wait_ge(r_made, i + 1)
                if prev:
                    act.wait_ge(k_made, i * T)
                for t in range(T):
                    nc.scalar.activation(a_l[:, t], bank[GRAM_L[t // J]][:, N * (t % J):N * (t % J) + N], ACT.Relu,
                                         scale=r_l[:, t:t + 1]).then_inc(al_out, 1)
                for t in range(T):
                    act.wait_ge(diag_g, i * PAIR + t // J + 1)
                    nc.scalar.activation(a_g[:, t], bank[GRAM_G[t // J]][:, N * (t % J):N * (t % J) + N],
                                         ACT.Identity, bias=norm2[:, 1, t:t + 1], scale=-2.0).then_inc(ag_out, 1)
                val_his(i, (0, 1))
                if norm_ahead:
                    norm1(i + 1)
                if prev:
                    act.wait_ge(al_made, i * T)
                for n, row in enumerate((row_r, row_sq)):
                    act.wait_ge(rows_ready, i * 2 + n + 1)
                    nc.scalar.copy(row[:], bank[ROWS[n]][:]).then_inc(rows_out, 1)
                val_his(i, (2, 3))
                if norm_ahead:
                    ht_his(i + 1)
                if prev:
                    norm2_out(i - 1)

            act.wait_ge(consts_loaded, 64)
            nc.scalar.activation(scal[:, 2:3], scal[:, 0:1], ACT.Exp, scale=-1.0).then_inc(gates_exp, 1)
            nc.scalar.activation(scal[:, 3:4], scal[:, 1:2], ACT.Exp).then_inc(gates_exp, 1)
            act.wait_ge(wl_loaded, 16)
            hi(wl_s[0][:], wl_raw).then_inc(weights_hi, 1)
            act.wait_ge(wg_loaded, 16)
            hi(wg_s[0][:], wg_raw).then_inc(weights_hi, 1)
            norm1(0)
            for c in range(C):
                act.wait_ge(wvo_ready, c + 1)
                hi(wvo_s[0][:, c], bank[HT[c]][:]).then_inc(wvo_hi, 1)
            ht_his(0)
            body(0, True)
            body(1, True)
            with act.Fori(2, G - 1) as i:
                body(i, True)
            body(G - 1, False)
            exps(G - 1)
            scale_lang(G - 1)
            kt_his(G - 1)
            norm2_out(G - 1)

        @block.vector
        def _(dve):
            def lo(dst, src, hi_part):
                return nc.vector.tensor_tensor(dst, src, hi_part.bitcast(F32), ALU.subtract)

            def layer_stats(k, t, src, stats, mv, summed, stats_made, mean_made):
                dve.wait_ge(summed, k * T + t + 1)
                nc.vector.bn_stats(stats[:, t, :], src[:, t]).then_inc(stats_made, 1)
                dve.wait_ge(stats_made, k * T + t + 1)
                dve.nop(nofuse=True)
                nc.vector.bn_aggr(mv[:, t, :], stats[:, t, :]).then_inc(mean_made, 1)

            def mix_outs(k):
                for t in range(T):
                    dve.wait_ge(mix_ready, k * T + t + 1)
                    if later(k):
                        dve.wait_ge(h_ready, (k - 1) * T + t + 1)
                    nc.vector.tensor_tensor(mixed[:, t], bank[MIX[t]][:], bias_b[:], ALU.add).then_inc(mix_out, 1)
                    layer_stats(k, t, mixed, stats1, mv1, mix_out, stats1_made, mean1_made)

            def ht_los(k):
                for c in range(C):
                    dve.wait_ge(ht_hi, k * C + c + 1)
                    lo(h_t[1][:, c], bank[HT[c]][:], h_t[0][:, c]).then_inc(ht_split, 1)

            def lang_affinity(i):
                dve.wait_ge(rows_out, i * 2 + 1)
                for t in range(T):
                    dve.wait_ge(al_masked, i * PAIR + t // J + 1)
                    nc.vector.scalar_tensor_tensor(a_l[:, t], a_l[:, t], 1.0, row_r[:, N * (t // J):N * (t // J) + N],
                                                   ALU.mult, ALU.mult, accum_out=deg[:, 0, t:t + 1]).then_inc(al_made, 1)

            def grav_affinity(i):
                for t in range(T):
                    dve.wait_ge(exp_made, i * PAIR + t // J + 1)
                    nc.vector.scalar_tensor_tensor(a_g[:, t], a_g[:, t], 1.0, mask[:, t % J],
                                                   ALU.min, ALU.mult, accum_out=deg[:, 1, t:t + 1]).then_inc(ag_made, 1)

            def degrees(i):
                dve.wait_ge(al_made, i * T + T)
                dve.wait_ge(ag_made, i * T + T)
                nc.vector.tensor_scalar(deg_max[:], deg[:], EPS, None, ALU.max).then_inc(coef_step, 1)
                dve.wait_ge(coef_step, i * 3 + 1)
                nc.vector.reciprocal(deg_inv[:], deg_max[:]).then_inc(coef_step, 1)
                dve.wait_ge(coef_step, i * 3 + 2)
                nc.vector.tensor_tensor(coef[:], deg_inv[:], branch_w[:], ALU.mult).then_inc(coef_step, 1)

            def build_k(i):
                if later(i - 1):
                    dve.wait_ge(kt_ready, i * PAIR)
                dve.wait_ge(coef_step, i * 3 + 3)
                for t in range(T):
                    dve.wait_ge(al_scaled, i * T + t + 1)
                    nc.vector.scalar_tensor_tensor(k_nm[:, t], a_g[:, t], coef[:, 1, t:t + 1], a_l[:, t],
                                                   ALU.mult, ALU.add).then_inc(k_made, 1)

            def diagonals(i, which, banks, ready, done):
                if later(i):
                    dve.wait_ge(done, i * PAIR)
                for b in range(PAIR):
                    dve.wait_ge(ready, i * PAIR + b + 1)
                    blocks = bank[banks[b]][:].rearrange("p (a c) -> p a c", c=P)[:, 0:4:3, :]
                    nc.vector.tensor_tensor(diag[:, which * PAIR + b], blocks, ident[:], ALU.mult).then_inc(diag_cut, 1)
                    dve.wait_ge(diag_cut, i * 2 * PAIR + which * PAIR + b + 1)
                    nc.vector.reduce_sum(norm2[:, which, J * b:J * b + J], diag[:, which * PAIR + b], axis=AX_X).then_inc(done, 1)

            def kt_los(i):
                for b in range(PAIR):
                    dve.wait_ge(kt_hi, i * PAIR + b + 1)
                    lo(k_t[1][:, J * b:J * b + J], bank[KT[b]][:].rearrange("p (j n) -> p j n", j=J),
                       k_t[0][:, J * b:J * b + J]).then_inc(kt_split, 1)

            def residuals(i):
                dve.wait_ge(h_saved, i + 1)
                if later(i):
                    dve.wait_ge(stored, i * 16)
                for t in range(T):
                    dve.wait_ge(agg_ready, i * T + t + 1)
                    nc.vector.tensor_tensor(y[:, t], bank[AGG[t]][:], h_res[:, t], ALU.add).then_inc(y_sum, 1)
                    layer_stats(i, t, y, stats2, mv2, y_sum, stats2_made, mean2_made)

            def body(i, mix_ahead, norm_ahead):
                prev = later(i)
                for e in range(C):
                    dve.wait_ge(zl_hi, i * C + e + 1)
                    lo(zl_t[1][:, e], bank[ZL[e]][:], zl_t[0][:, e]).then_inc(zl_split, 1)
                    if prev and e == 0:
                        lang_affinity(i - 1)
                    if prev and e == 1:
                        grav_affinity(i - 1)
                        degrees(i - 1)
                for e in range(C):
                    dve.wait_ge(zg_hi, i * C + e + 1)
                    lo(zg_t[1][:, e], bank[ZG[e]][:], zg_t[0][:, e]).then_inc(zg_split, 1)
                    if prev and e == 1:
                        build_k(i - 1)
                if prev:
                    dve.wait_ge(r_guarded, i)
                diagonals(i, 0, GRAM_L, gram_l_ready, diag_l)
                if prev:
                    kt_los(i - 1)
                    dve.wait_ge(ag_out, i * T)
                    dve.wait_ge(rows_ready, i * 2)
                diagonals(i, 1, GRAM_G, gram_g_ready, diag_g)
                if prev:
                    residuals(i - 1)
                for t in range(T):
                    dve.wait_ge(v_hi, i * T + t + 1)
                    lo(v_s[1][:, t], bank[VAL[t]][:], v_s[0][:, t]).then_inc(v_split, 1)
                if norm_ahead:
                    ht_los(i + 1)
                if mix_ahead:
                    mix_outs(i + 2)

            dve.wait_ge(consts_loaded, 64)
            nc.vector.tensor_tensor(mix_w[:], mask[:], mask[:], ALU.mult).then_inc(mix_made, 1)
            dve.wait_ge(mix_made, 1)
            dve.wait_ge(ident_made, 2)
            mix_diag = mix_w[:].rearrange("p j (a c) -> p (j a) c", c=P)[:, 0:4:3, :]
            nc.vector.tensor_tensor(mix_diag, mix_diag, ident[:], ALU.add).then_inc(mix_made, 1)
            dve.wait_ge(mix_made, 2)
            nc.vector.tensor_copy(mix_s[0][:], mix_w[:]).then_inc(mix_made, 1)
            dve.wait_ge(mix_made, 3)
            lo(mix_s[1][:], mix_w[:], mix_s[0][:]).then_inc(mix_made, 1)
            dve.wait_ge(gates_exp, 2)
            nc.vector.tensor_scalar(scal[:, 4:5], scal[:, 2:3], 1.0, None, ALU.add).then_inc(gates_step, 1)
            nc.vector.tensor_tensor(scal[:, 5:6], scal[:, 3:4], scal[:, 3:4], ALU.mult).then_inc(gates_step, 1)
            dve.wait_ge(gates_step, 2)
            nc.vector.reciprocal(scal[:, 2:3], scal[:, 4:5]).then_inc(gates_step, 1)
            nc.vector.reciprocal(scal[:, 6:7], scal[:, 5:6]).then_inc(gates_step, 1)
            dve.wait_ge(gates_step, 4)
            nc.vector.tensor_scalar(branch_w[:, 0], branch_w[:, 0], scal[:, 2:3], None, ALU.mult).then_inc(gates_step, 1)
            nc.vector.tensor_scalar(d2_scale, scal[:, 6:7], -0.5, None, ALU.mult).then_inc(gates_step, 1)
            dve.wait_ge(gates_step, 5)
            nc.vector.tensor_scalar(branch_w[:, 1], branch_w[:, 0], -1.0, 1.0, ALU.mult, ALU.add).then_inc(gates_step, 1)
            dve.wait_ge(gates_step, 7)
            dve.wait_ge(weights_hi, 1)
            lo(wl_s[1][:], wl_raw, wl_s[0][:]).then_inc(weights_split, 1)
            dve.wait_ge(weights_split, 1)
            mix_outs(0)
            dve.wait_ge(weights_hi, 2)
            lo(wg_s[1][:], wg_raw, wg_s[0][:]).then_inc(weights_split, 1)
            for c in range(C):
                dve.wait_ge(wvo_hi, c + 1)
                lo(wvo_s[1][:, c], bank[HT[c]][:], wvo_s[0][:, c]).then_inc(wvo_split, 1)
            ht_los(0)
            mix_outs(1)
            body(0, True, True)
            body(1, True, True)
            with dve.Fori(2, G - 2) as i:
                body(i, True, True)
            body(G - 2, False, True)
            body(G - 1, False, False)
            lang_affinity(G - 1)
            grav_affinity(G - 1)
            degrees(G - 1)
            build_k(G - 1)
            kt_los(G - 1)
            residuals(G - 1)

        @block.tensor
        def _(pe):
            def product(dst, steps):
                n = 0
                for lhs, rhs in steps:
                    for a, b in PRODUCTS:
                        last = nc.tensor.matmul(dst, lhs(a), rhs(b), start=(n == 0), stop=(n == 3 * len(steps) - 1))
                        n += 1
                return last

            def mix(t):
                b, m = t // J, t % J
                steps = [(lambda s, j=j: mix_s[s][:, j, P * m:P * m + P], lambda s, j=j: x_s[s][:, J * b + j, :])
                         for j in range(J)]
                product(bank[MIX[t]][:], steps).then_inc(mix_ready, 1)

            def transpose_h(c):
                for t in range(T):
                    last = nc.tensor.transpose(bank[HT[c]][:, P * t:P * t + P], h_new[:, t, P * c:P * c + P],
                                               ident[:, 0])
                last.then_inc(ht_ready, 1)

            def projection(banks, e, w, ready):
                steps = [(lambda s, c=c: w[s][:, c, P * e:P * e + P], lambda s, c=c: h_t[s][:, c, :]) for c in range(C)]
                product(bank[banks[e]][:], steps).then_inc(ready, 1)

            def gram(banks, z, ready):
                for b in range(PAIR):
                    for j in range(J):
                        q = J * b + j
                        steps = [(lambda s, c=c: z[s][:, c, P * q:P * q + P], lambda s, c=c: z[s][:, c, N * b:N * b + N])
                                 for c in range(C)]
                        last = product(bank[banks[b]][:, N * j:N * j + N], steps)
                    last.then_inc(ready, 1)

            def value(t):
                steps = [(lambda s, c=c: h_t[s][:, c, P * t:P * t + P], lambda s, c=c: wvo_s[s][:, c, :]) for c in range(C)]
                product(bank[VAL[t]][:], steps).then_inc(v_ready, 1)

            def rows(i):
                pe.wait_ge(r_made, i + 1)
                pe.wait_ge(diag_g, i * PAIR + PAIR)
                for n, column in enumerate((r_l[:], norm2[:, 1, :])):
                    pe.wait_ge(al_out, i * T + J * n + J)
                    for t in range(T):
                        last = nc.tensor.transpose(bank[ROWS[n]][:, P * t:P * t + P],
                                                   column[:, t:t + 1].to_broadcast([P, P]), ident[:, 0])
                    last.then_inc(rows_ready, 1)

            def transpose_k(i):
                for b in range(PAIR):
                    pe.wait_ge(k_made, i * T + J * b + J)
                    for m in range(J):
                        for j in range(J):
                            last = nc.tensor.transpose(bank[KT[b]][:, N * m + P * j:N * m + P * j + P],
                                                       k_nm[:, J * b + j, P * m:P * m + P], ident[:, 0])
                    last.then_inc(kt_ready, 1)

            def aggregate(i):
                pe.wait_ge(v_split, i * T + T)
                for t in range(T):
                    b, j = t // J, t % J
                    pe.wait_ge(kt_split, i * PAIR + b + 1)
                    steps = [(lambda s, m=m: k_t[s][:, J * b + m, P * j:P * j + P], lambda s, m=m: v_s[s][:, J * b + m, :])
                             for m in range(J)]
                    product(bank[AGG[t]][:], steps).then_inc(agg_ready, 1)

            def body(i, mix_ahead, norm_ahead):
                prev = later(i)
                pe.wait_ge(ht_split, i * C + C)
                if not prev:
                    pe.wait_ge(weights_split, 1)
                for e in range(C):
                    if norm_ahead:
                        pe.wait_ge(mix_out, i * T + T + e + 1)
                    elif e < 2:
                        pe.wait_ge(rows_out, i * 2 - 1 + e)
                    else:
                        pe.wait_ge(v_split, i * T - T + e + 1)
                    projection(ZL, e, wl_s, zl_ready)
                if not prev:
                    pe.wait_ge(weights_split, 2)
                for e in range(C):
                    projection(ZG, e, wg_s, zg_ready)
                pe.wait_ge(zl_split, i * C + C)
                gram(GRAM_L, zl_t, gram_l_ready)
                if prev:
                    transpose_k(i - 1)
                pe.wait_ge(zg_split, i * C + C)
                gram(GRAM_G, zg_t, gram_g_ready)
                if prev:
                    aggregate(i - 1)
                for t in range(T):
                    if prev:
                        pe.wait_ge(y_sum, i * T - T + t + 1)
                    value(t)
                    if t == 1:
                        rows(i)
                if norm_ahead:
                    pe.wait_ge(h_ready, i * T + 2 * T)
                    for c in range(C):
                        if c < 2:
                            pe.wait_ge(ag_out, i * T + J * c + J)
                        else:
                            pe.wait_ge(v_split, i * T + c - 1)
                        transpose_h(c)
                if mix_ahead:
                    pe.wait_ge(x_split, i + 3)
                    for t in range(T):
                        if t < 2:
                            pe.wait_ge(rows_out, i * 2 + t + 1)
                        else:
                            pe.wait_ge(v_split, i * T + t + 1)
                        mix(t)

            pe.wait_ge(mix_made, 4)
            pe.wait_ge(x_split, 1)
            for t in range(T):
                mix(t)
            pe.wait_ge(vo_loaded, 32)
            for c in range(C):
                for v in range(C):
                    last = nc.tensor.matmul(bank[HT[c]][:], wv_raw[:, v, P * c:P * c + P], wo_raw[:, v, :],
                                            start=(v == 0), stop=(v == C - 1))
                last.then_inc(wvo_ready, 1)
            pe.wait_ge(h_ready, T)
            for c in range(C):
                pe.wait_ge(wvo_split, c + 1)
                transpose_h(c)
            pe.wait_ge(x_split, 2)
            for t in range(T):
                pe.wait_ge(mix_out, t + 1)
                mix(t)
            body(0, True, True)
            body(1, True, True)
            with pe.Fori(2, G - 2) as i:
                body(i, True, True)
            body(G - 2, False, True)
            body(G - 1, False, False)
            pe.wait_ge(v_split, G * T)
            transpose_k(G - 1)
            aggregate(G - 1)

    return nc


def kernel(x, adj, L0_gnn_bias, L1_gnn_W_lang, L1_gnn_W_grav, L1_gnn_W_V, L1_gnn_W_O, L1_gnn_gate_logit,
           L1_gnn_log_sigma):
    import numpy as np
    import concourse.bacc as bacc
    from concourse.bass_utils import run_bass_kernel_spmd

    arrays = {
        "x": np.ascontiguousarray(x),
        "adj": np.ascontiguousarray(adj),
        "bias": np.ascontiguousarray(L0_gnn_bias).reshape(1, -1),
        "w_lang_t": np.ascontiguousarray(np.asarray(L1_gnn_W_lang).T),
        "w_grav_t": np.ascontiguousarray(np.asarray(L1_gnn_W_grav).T),
        "w_v": np.ascontiguousarray(L1_gnn_W_V),
        "w_o_t": np.ascontiguousarray(np.asarray(L1_gnn_W_O).T),
        "gate": np.ascontiguousarray(L1_gnn_gate_logit).reshape(1, 1),
        "log_sigma": np.ascontiguousarray(L1_gnn_log_sigma).reshape(1, 1),
    }
    nc = bacc.Bacc("TRN2", target_bir_lowering=False, num_devices=1)
    args = [nc.dram_tensor(name, a.shape, F32, kind="ExternalInput").ap() for name, a in arrays.items()]
    out = nc.dram_tensor("out", arrays["x"].shape, F32, kind="ExternalOutput").ap()
    bass_adj_resnorm_kernel(nc, *args, out)
    return run_bass_kernel_spmd(nc, [arrays], core_ids=[0]).results[0]["out"]
```

```python
from contextlib import ExitStack

import concourse.bass as bass
from concourse import mybir

F32 = mybir.dt.float32
F32R = mybir.dt.float32r
ALU = mybir.AluOpType
ACT = mybir.ActivationFunctionType
AX_X = mybir.AxisListType.X

P = 128
LN_EPS = 1e-5
EPS = 1e-8

PRODUCTS = ((0, 0), (0, 1), (1, 0))

GRAM_PRODUCTS = ((0, 0), (0, 1))


def bass_adj_resnorm_kernel(nc, x, adj, bias, w_lang_t, w_grav_t, w_v, w_o_t, gate, log_sigma, out):
    B, N, D = x.shape
    PAIR = 2
    J = N // P
    T = PAIR * J
    C = D // P
    TOK = PAIR * N
    G = B // PAIR
    assert N == 2 * P and D == 512 and TOK == 512 and T == 4 and C == 4 and G >= 5

    x_pairs = x.rearrange("b n f -> (b n) f").rearrange("(g t p) f -> g p t f", t=T, p=P)
    out_pairs = out.rearrange("b n f -> (b n) f").rearrange("(g t p) f -> g p t f", t=T, p=P)

    with ExitStack() as ctx:
        def sb(name, shape, dt=F32):
            return ctx.enter_context(nc.sbuf_tensor(name, shape, dt))

        def sem(name):
            return ctx.enter_context(nc.semaphore(name))

        def split(name, shape):
            return [sb(name + "_hi", shape, F32R), sb(name + "_lo", shape, F32R)]

        x_raw = sb("x_raw", [P, T, D])
        x_s = split("x", [P, T, D])
        mixed = sb("mixed", [P, T, D])
        h_new = sb("h_new", [P, T, D])
        h_res = sb("h_res", [P, T, D])
        h_t = split("h_t", [P, C, TOK])
        zl_t = split("zl_t", [P, C, TOK])
        zg_t = split("zg_t", [P, C, TOK])
        v_s = split("v", [P, T, D])
        y = sb("y", [P, T, D])
        wl_s = split("wl", [P, C, D])
        wg_s = split("wg", [P, C, D])
        wvo_s = split("wvo", [P, C, D])
        mix_s = split("mix", [P, J, N])
        mix_w = sb("mix_w", [P, J, N])
        mask = sb("mask", [P, J, N])
        bias_b = sb("bias_b", [P, D])
        ident = sb("ident", [P, J, P])
        aff = sb("aff", [P, 2, T, N])
        a_l, a_g = aff[:, 0], aff[:, 1]
        k_nm = sb("k_nm", [P, T, N])
        k_t = split("k_t", [P, T, N])
        row_r = sb("row_r", [P, T * P])
        diag = sb("diag", [P, 2 * PAIR, J, P])
        norm2 = sb("norm2", [P, 2, T])
        guarded = sb("guarded", [P, T])
        r_l = sb("r_l", [P, T])
        deg = sb("deg", [P, 2, T])
        deg_max = sb("deg_max", [P, 2, T])
        deg_inv = sb("deg_inv", [P, 2, T])
        coef = sb("coef", [P, 2, T])
        branch_w = sb("branch_w", [P, 2, T])
        stats1 = sb("stats1", [P, T, 6])
        mv1 = sb("mv1", [P, T, 2])
        rstd1 = sb("rstd1", [P, 4, T])
        stats2 = sb("stats2", [P, T, 6])
        mv2 = sb("mv2", [P, T, 2])
        rstd2 = sb("rstd2", [P, 4, T])
        minus_half = sb("minus_half", [P, T])
        scal = sb("scal", [P, 8])
        d2_scale = scal[:, 7:8]

        bank = [ctx.enter_context(nc.psum_tensor(f"bank{i}", [P, 512], F32)) for i in range(8)]

        wl_raw, wg_raw, wv_raw = mixed[:], h_res[:], y[:]
        wo_raw = aff[:].rearrange("p a t n -> p (a t n)").rearrange("p (c e) -> p c e", c=C)

        ZL, ZG, GRAM_L, KT, GRAM_G = (0, 1, 2, 3), (4, 5, 6, 7), (0, 1), (2, 3), (4, 5)
        AGG, SYM_L, VAL, SYM_G, ROWS = (6, 7, 2, 3), (0, 1), (6, 7, 2, 3), (4, 5), 0
        HT, MIX = (4, 5, 6, 7), (0, 1, 2, 3)

        consts_loaded = sem("consts_loaded")
        wl_loaded = sem("wl_loaded")
        wg_loaded = sem("wg_loaded")
        vo_loaded = sem("vo_loaded")
        ident_made = sem("ident_made")
        gates_exp = sem("gates_exp")
        gates_step = sem("gates_step")
        mix_made = sem("mix_made")
        weights_hi = sem("weights_hi")
        weights_split = sem("weights_split")
        wvo_ready = sem("wvo_ready")
        wvo_hi = sem("wvo_hi")
        wvo_split = sem("wvo_split")
        mask_made = sem("mask_made")

        x_loaded = sem("x_loaded")
        x_hi_made = sem("x_hi_made")
        x_split = sem("x_split")
        mix_ready = sem("mix_ready")
        mix_out = sem("mix_out")
        stats1_made = sem("stats1_made")
        mean1_made = sem("mean1_made")
        rstd1_step = sem("rstd1_step")
        h_ready = sem("h_ready")
        h_saved = sem("h_saved")
        ht_ready = sem("ht_ready")
        ht_hi = sem("ht_hi")
        ht_split = sem("ht_split")
        zl_ready = sem("zl_ready")
        zl_hi = sem("zl_hi")
        zl_split = sem("zl_split")
        zg_ready = sem("zg_ready")
        zg_hi = sem("zg_hi")
        zg_split = sem("zg_split")
        gram_l_ready = sem("gram_l_ready")
        gram_g_ready = sem("gram_g_ready")
        diag_cut = sem("diag_cut")
        diag_l = sem("diag_l")
        diag_g = sem("diag_g")
        r_guarded = sem("r_guarded")
        r_made = sem("r_made")
        sl_out = sem("sl_out")
        sg_out = sem("sg_out")
        sl_t_ready = sem("sl_t_ready")
        sg_t_ready = sem("sg_t_ready")
        rows_ready = sem("rows_ready")
        rows_out = sem("rows_out")
        gl_made = sem("gl_made")
        d2_made = sem("d2_made")
        al_masked = sem("al_masked")
        exp_made = sem("exp_made")
        al_made = sem("al_made")
        ag_made = sem("ag_made")
        coef_step = sem("coef_step")
        al_scaled = sem("al_scaled")
        k_made = sem("k_made")
        kt_ready = sem("kt_ready")
        kt_hi = sem("kt_hi")
        kt_split = sem("kt_split")
        v_ready = sem("v_ready")
        v_hi = sem("v_hi")
        v_split = sem("v_split")
        agg_ready = sem("agg_ready")
        y_sum = sem("y_sum")
        stats2_made = sem("stats2_made")
        mean2_made = sem("mean2_made")
        rstd2_step = sem("rstd2_step")
        y_ready = sem("y_ready")
        stored = sem("stored")

        def later(i):
            return not (isinstance(i, int) and i <= 0)

        block = ctx.enter_context(nc.Block())

        @block.sync
        def _(sp):
            def load_x(k):
                if later(k):
                    sp.wait_ge(x_split, k)
                sp.dma_start(x_raw[:], x_pairs[bass.ds(k, 1)].rearrange("g p t f -> p (g t) f")).then_inc(x_loaded, 16)

            def store(k):
                sp.wait_ge(y_ready, k * T + T)
                sp.dma_start(out_pairs[bass.ds(k, 1)].rearrange("g p t f -> p (g t) f"), y[:]).then_inc(stored, 16)

            load_x(0)
            sp.dma_start(mask[:], adj.rearrange("(j p) m -> p j m", p=P)).then_inc(consts_loaded, 16)
            sp.dma_start(bias_b[:], bias.broadcast_to([P, D])).then_inc(consts_loaded, 16)
            sp.dma_start(scal[:, 0:1], gate.broadcast_to([P, 1])).then_inc(consts_loaded, 16)
            sp.dma_start(scal[:, 1:2], log_sigma.broadcast_to([P, 1])).then_inc(consts_loaded, 16)
            sp.dma_start(wl_raw, w_lang_t.rearrange("(c p) e -> p c e", p=P)).then_inc(wl_loaded, 16)
            sp.dma_start(wg_raw, w_grav_t.rearrange("(c p) e -> p c e", p=P)).then_inc(wg_loaded, 16)
            sp.dma_start(wv_raw, w_v.rearrange("(c p) e -> p c e", p=P)).then_inc(vo_loaded, 16)
            sp.dma_start(wo_raw, w_o_t.rearrange("(c p) e -> p c e", p=P)).then_inc(vo_loaded, 16)
            load_x(1)
            load_x(2)
            load_x(3)
            with sp.Fori(1, G - 3) as i:
                store(i - 1)
                load_x(i + 3)
            for k in range(G - 4, G):
                store(k)
            sp.wait_ge(stored, 16 * G)


        @block.gpsimd
        def _(pool):
            def split_x(k):
                pool.wait_ge(x_hi_made, k + 1)
                nc.gpsimd.tensor_tensor(x_s[1][:], x_raw[:], x_s[0][:].bitcast(F32), ALU.subtract).then_inc(x_split, 1)

            def norm_factors(k, mv, f, mean_made, step):
                pool.wait_ge(mean_made, k * T + T)
                pool.nop(nofuse=True)
                nc.gpsimd.tensor_scalar(f[:, 0, :], mv[:, :, 1], LN_EPS, None, ALU.add).then_inc(step, 1)
                nc.gpsimd.tensor_scalar(f[:, 1, :], mv[:, :, 0], -1.0, None, ALU.mult).then_inc(step, 1)
                pool.wait_ge(step, k * 4 + 1)
                nc.gpsimd.tensor_tensor(f[:, 2, :], f[:, 0, :], minus_half[:], ALU.pow).then_inc(step, 1)
                pool.wait_ge(step, k * 4 + 3)
                nc.gpsimd.tensor_tensor(f[:, 3, :], f[:, 1, :], f[:, 2, :], ALU.mult).then_inc(step, 1)

            def lang_norms(i):
                pool.wait_ge(diag_l, i * PAIR + PAIR)
                pool.nop(nofuse=True)
                nc.gpsimd.tensor_scalar(guarded[:], norm2[:, 0, :], EPS * EPS, None, ALU.max).then_inc(r_guarded, 1)
                pool.wait_ge(r_guarded, i + 1)
                if later(i):
                    pool.wait_ge(rows_ready, i)
                    pool.wait_ge(al_made, i * T)
                nc.gpsimd.tensor_tensor(r_l[:], guarded[:], minus_half[:], ALU.pow).then_inc(r_made, 1)

            def save_h(i):
                if not later(i):
                    pool.wait_ge(weights_split, 2)
                for t in range(T):
                    if later(i):
                        pool.wait_ge(y_sum, i * T - T + t + 1)
                        pool.nop(nofuse=True)
                    nc.gpsimd.tensor_copy(h_res[:, t], h_new[:, t]).then_inc(h_saved, 1)

            def body(i, mix_ahead, norm_ahead):
                if norm_ahead:
                    norm_factors(i + 1, mv1, rstd1, mean1_made, rstd1_step)
                if mix_ahead:
                    split_x(i + 2)
                lang_norms(i)
                save_h(i)
                if later(i):
                    norm_factors(i - 1, mv2, rstd2, mean2_made, rstd2_step)

            nc.gpsimd.memset(minus_half[:], -0.5)
            nc.gpsimd.memset(branch_w[:], 1.0)
            nc.gpsimd.memset(ident[:], 0.0).then_inc(ident_made, 1)
            pool.wait_ge(ident_made, 1)
            nc.gpsimd.affine_select(out=ident[:], in_=ident[:], compare_op=ALU.not_equal, fill=1.0, base=0,
                                    pattern=[[0, J], [-1, P]], channel_multiplier=1).then_inc(ident_made, 1)
            split_x(0)
            pool.wait_ge(mix_made, 1)
            nc.gpsimd.affine_select(out=mask[:], in_=mask[:], compare_op=ALU.not_equal, fill=0.0, base=0,
                                    pattern=[[P, J], [-1, N]], channel_multiplier=1).then_inc(mask_made, 1)
            norm_factors(0, mv1, rstd1, mean1_made, rstd1_step)
            split_x(1)
            body(0, True, True)
            body(1, True, True)
            with pool.Fori(2, G - 2) as i:
                body(i, True, True)
            body(G - 2, False, True)
            body(G - 1, False, False)
            norm_factors(G - 1, mv2, rstd2, mean2_made, rstd2_step)

        @block.scalar
        def _(act):
            def hi(dst, src):
                return nc.scalar.activation(dst, src, ACT.Identity)

            def x_his(k):
                act.wait_ge(x_loaded, k * 16 + 16)
                if later(k):
                    act.wait_ge(mix_ready, k * T)
                hi(x_s[0][:], x_raw[:]).then_inc(x_hi_made, 1)

            def hi_of_double(dst, src):
                return nc.scalar.activation(dst, src, ACT.Identity, scale=0.5)

            def norm1(k):
                act.wait_ge(rstd1_step, k * 4 + 4)
                if later(k):
                    act.wait_ge(ht_ready, k * C)
                for t in range(T):
                    if later(k):
                        act.wait_ge(h_saved, k * T - T + t + 1)
                    nc.scalar.activation(h_new[:, t], mixed[:, t], ACT.Identity, bias=rstd1[:, 3, t:t + 1],
                                         scale=rstd1[:, 2, t:t + 1]).then_inc(h_ready, 1)

            def norm2_out(k):
                act.wait_ge(rstd2_step, k * 4 + 4)
                for t in range(T):
                    nc.scalar.activation(y[:, t], y[:, t], ACT.Identity, bias=rstd2[:, 3, t:t + 1],
                                         scale=rstd2[:, 2, t:t + 1]).then_inc(y_ready, 1)

            def ht_his(k):
                if later(k):
                    act.wait_ge(v_ready, k * T)
                for c in range(C):
                    act.wait_ge(ht_ready, k * C + c + 1)
                    hi(h_t[0][:, c], bank[HT[c]][:]).then_inc(ht_hi, 1)

            def val_his(i, ts):
                if later(i):
                    act.wait_ge(agg_ready, i * T)
                for t in ts:
                    act.wait_ge(v_ready, i * T + t + 1)
                    hi(v_s[0][:, t], bank[VAL[t]][:]).then_inc(v_hi, 1)

            def exps(i):
                for b in range(PAIR):
                    act.wait_ge(d2_made, i * PAIR + b + 1)
                    nc.scalar.activation(a_g[:, J * b:J * b + J], a_g[:, J * b:J * b + J], ACT.Exp,
                                         scale=d2_scale).then_inc(exp_made, 1)

            def scale_lang(i):
                act.wait_ge(coef_step, i * 3 + 3)
                for t in range(T):
                    nc.scalar.activation(a_l[:, t], a_l[:, t], ACT.Identity,
                                         scale=coef[:, 0, t:t + 1]).then_inc(al_scaled, 1)

            def kt_his(i):
                if later(i - 1):
                    act.wait_ge(agg_ready, i * T)
                for b in range(PAIR):
                    act.wait_ge(kt_ready, i * PAIR + b + 1)
                    hi(k_t[0][:, J * b:J * b + J], bank[KT[b]][:]).then_inc(kt_hi, 1)

            def body(i, mix_ahead, norm_ahead):
                prev = later(i)
                if prev:
                    act.wait_ge(gram_l_ready, i * PAIR)
                for e in range(C):
                    act.wait_ge(zl_ready, i * C + e + 1)
                    hi_of_double(zl_t[0][:, e], bank[ZL[e]][:]).then_inc(zl_hi, 1)
                    if prev and e == 0:
                        exps(i - 1)
                    if mix_ahead and e == 2:
                        x_his(i + 2)
                if prev:
                    act.wait_ge(gram_g_ready, i * PAIR)
                for e in range(C):
                    act.wait_ge(zg_ready, i * C + e + 1)
                    hi_of_double(zg_t[0][:, e], bank[ZG[e]][:]).then_inc(zg_hi, 1)
                    if prev and e == 1:
                        scale_lang(i - 1)
                if prev:
                    act.wait_ge(k_made, i * T)
                for b in range(PAIR):
                    act.wait_ge(diag_l, i * PAIR + b + 1)
                    nc.scalar.copy(a_l[:, J * b:J * b + J].rearrange("p j n -> p (j n)"),
                                   bank[GRAM_L[b]][:]).then_inc(sl_out, 1)
                if prev:
                    kt_his(i - 1)
                for t in range(T):
                    act.wait_ge(diag_g, i * PAIR + t // J + 1)
                    nc.scalar.activation(a_g[:, t], bank[GRAM_G[t // J]][:, N * (t % J):N * (t % J) + N],
                                         ACT.Identity, bias=norm2[:, 1, t:t + 1], scale=-1.0).then_inc(sg_out, 1)
                val_his(i, (0, 1))
                if norm_ahead:
                    norm1(i + 1)
                if prev:
                    act.wait_ge(al_made, i * T)
                act.wait_ge(rows_ready, i + 1)
                nc.scalar.activation(row_r[:], bank[ROWS][:], ACT.Copy, scale=0.5).then_inc(rows_out, 1)
                val_his(i, (2, 3))
                if norm_ahead:
                    ht_his(i + 1)
                if prev:
                    norm2_out(i - 1)

            act.wait_ge(consts_loaded, 64)
            nc.scalar.activation(scal[:, 2:3], scal[:, 0:1], ACT.Exp, scale=-1.0).then_inc(gates_exp, 1)
            nc.scalar.activation(scal[:, 3:4], scal[:, 1:2], ACT.Exp).then_inc(gates_exp, 1)
            x_his(0)
            act.wait_ge(wl_loaded, 16)
            nc.scalar.activation(wl_s[0][:], wl_raw, ACT.Identity, scale=2.0).then_inc(weights_hi, 1)
            act.wait_ge(wg_loaded, 16)
            nc.scalar.activation(wg_s[0][:], wg_raw, ACT.Identity, scale=2.0).then_inc(weights_hi, 1)
            norm1(0)
            x_his(1)
            for c in range(C):
                act.wait_ge(wvo_ready, c + 1)
                hi(wvo_s[0][:, c], bank[HT[c]][:]).then_inc(wvo_hi, 1)
            ht_his(0)
            body(0, True, True)
            body(1, True, True)
            with act.Fori(2, G - 2) as i:
                body(i, True, True)
            body(G - 2, False, True)
            body(G - 1, False, False)
            exps(G - 1)
            scale_lang(G - 1)
            kt_his(G - 1)
            norm2_out(G - 1)

        @block.vector
        def _(dve):
            def lo(dst, src, hi_part):
                return nc.vector.tensor_tensor(dst, src, hi_part.bitcast(F32), ALU.subtract)

            def layer_stats(k, t, src, stats, mv, summed, stats_made, mean_made):
                dve.wait_ge(summed, k * T + t + 1)
                nc.vector.bn_stats(stats[:, t, :], src[:, t]).then_inc(stats_made, 1)
                dve.wait_ge(stats_made, k * T + t + 1)
                dve.nop(nofuse=True)
                nc.vector.bn_aggr(mv[:, t, :], stats[:, t, :]).then_inc(mean_made, 1)

            def mix_outs(k):
                for t in range(T):
                    dve.wait_ge(mix_ready, k * T + t + 1)
                    if later(k):
                        dve.wait_ge(h_ready, (k - 1) * T + t + 1)
                    nc.vector.tensor_tensor(mixed[:, t], bank[MIX[t]][:], bias_b[:], ALU.add).then_inc(mix_out, 1)
                    layer_stats(k, t, mixed, stats1, mv1, mix_out, stats1_made, mean1_made)

            def ht_los(k):
                for c in range(C):
                    dve.wait_ge(ht_hi, k * C + c + 1)
                    lo(h_t[1][:, c], bank[HT[c]][:], h_t[0][:, c]).then_inc(ht_split, 1)

            def lo_twice(dst, double, hi_part):
                return nc.vector.scalar_tensor_tensor(dst, hi_part.bitcast(F32), -2.0, double, ALU.mult, ALU.add)

            def symmetrize(i, part, banks, ready, done):
                for b in range(PAIR):
                    dve.wait_ge(ready, i * PAIR + b + 1)
                    flat = part[:, J * b:J * b + J].rearrange("p j n -> p (j n)")
                    nc.vector.tensor_tensor(flat, bank[banks[b]][:], flat, ALU.add).then_inc(done, 1)

            def mask_lang(i):
                for b in range(PAIR):
                    dve.wait_ge(gl_made, i * PAIR + b + 1)
                    nc.vector.scalar_tensor_tensor(a_l[:, J * b:J * b + J], a_l[:, J * b:J * b + J], 0.0, mask[:],
                                                   ALU.max, ALU.mult).then_inc(al_masked, 1)

            def lang_affinity(i):
                dve.wait_ge(rows_out, i + 1)
                for t in range(T):
                    dve.wait_ge(al_masked, i * PAIR + t // J + 1)
                    nc.vector.scalar_tensor_tensor(a_l[:, t], a_l[:, t], r_l[:, t:t + 1],
                                                   row_r[:, N * (t // J):N * (t // J) + N],
                                                   ALU.mult, ALU.mult, accum_out=deg[:, 0, t:t + 1]).then_inc(al_made, 1)

            def grav_affinity(i):
                for t in range(T):
                    dve.wait_ge(exp_made, i * PAIR + t // J + 1)
                    nc.vector.scalar_tensor_tensor(a_g[:, t], a_g[:, t], 1.0, mask[:, t % J],
                                                   ALU.min, ALU.mult, accum_out=deg[:, 1, t:t + 1]).then_inc(ag_made, 1)

            def degrees(i):
                dve.wait_ge(al_made, i * T + T)
                dve.wait_ge(ag_made, i * T + T)
                nc.vector.tensor_scalar(deg_max[:], deg[:], EPS, None, ALU.max).then_inc(coef_step, 1)
                dve.wait_ge(coef_step, i * 3 + 1)
                nc.vector.reciprocal(deg_inv[:], deg_max[:]).then_inc(coef_step, 1)
                dve.wait_ge(coef_step, i * 3 + 2)
                nc.vector.tensor_tensor(coef[:], deg_inv[:], branch_w[:], ALU.mult).then_inc(coef_step, 1)

            def build_k(i):
                if later(i - 1):
                    dve.wait_ge(kt_ready, i * PAIR)
                dve.wait_ge(coef_step, i * 3 + 3)
                for t in range(T):
                    dve.wait_ge(al_scaled, i * T + t + 1)
                    nc.vector.scalar_tensor_tensor(k_nm[:, t], a_g[:, t], coef[:, 1, t:t + 1], a_l[:, t],
                                                   ALU.mult, ALU.add).then_inc(k_made, 1)

            def diagonals(i, which, banks, ready, done):
                if later(i):
                    dve.wait_ge(done, i * PAIR)
                for b in range(PAIR):
                    dve.wait_ge(ready, i * PAIR + b + 1)
                    blocks = bank[banks[b]][:].rearrange("p (a c) -> p a c", c=P)[:, 0:4:3, :]
                    nc.vector.tensor_tensor(diag[:, which * PAIR + b], blocks, ident[:], ALU.mult).then_inc(diag_cut, 1)
                    dve.wait_ge(diag_cut, i * 2 * PAIR + which * PAIR + b + 1)
                    nc.vector.reduce_sum(norm2[:, which, J * b:J * b + J], diag[:, which * PAIR + b], axis=AX_X).then_inc(done, 1)

            def kt_los(i):
                for b in range(PAIR):
                    dve.wait_ge(kt_hi, i * PAIR + b + 1)
                    lo(k_t[1][:, J * b:J * b + J], bank[KT[b]][:].rearrange("p (j n) -> p j n", j=J),
                       k_t[0][:, J * b:J * b + J]).then_inc(kt_split, 1)

            def residuals(i):
                if later(i):
                    dve.wait_ge(stored, i * 16)
                for t in range(T):
                    dve.wait_ge(h_saved, i * T + t + 1)
                    dve.wait_ge(agg_ready, i * T + t + 1)
                    nc.vector.tensor_tensor(y[:, t], bank[AGG[t]][:], h_res[:, t], ALU.add).then_inc(y_sum, 1)
                    layer_stats(i, t, y, stats2, mv2, y_sum, stats2_made, mean2_made)

            def body(i, mix_ahead, norm_ahead):
                prev = later(i)
                for e in range(C):
                    dve.wait_ge(zl_hi, i * C + e + 1)
                    lo_twice(zl_t[1][:, e], bank[ZL[e]][:], zl_t[0][:, e]).then_inc(zl_split, 1)
                    if prev and e == 0:
                        lang_affinity(i - 1)
                    if prev and e == 1:
                        grav_affinity(i - 1)
                        degrees(i - 1)
                for e in range(C):
                    dve.wait_ge(zg_hi, i * C + e + 1)
                    lo_twice(zg_t[1][:, e], bank[ZG[e]][:], zg_t[0][:, e]).then_inc(zg_split, 1)
                    if prev and e == 1:
                        build_k(i - 1)
                if prev:
                    dve.wait_ge(r_guarded, i)
                diagonals(i, 0, GRAM_L, gram_l_ready, diag_l)
                if prev:
                    kt_los(i - 1)
                    dve.wait_ge(sg_out, i * T)
                diagonals(i, 1, GRAM_G, gram_g_ready, diag_g)
                if prev:
                    residuals(i - 1)
                symmetrize(i, a_l, SYM_L, sl_t_ready, gl_made)
                for t in range(T):
                    dve.wait_ge(v_hi, i * T + t + 1)
                    lo(v_s[1][:, t], bank[VAL[t]][:], v_s[0][:, t]).then_inc(v_split, 1)
                    if t == 1:
                        symmetrize(i, a_g, SYM_G, sg_t_ready, d2_made)
                        mask_lang(i)
                if norm_ahead:
                    ht_los(i + 1)
                if mix_ahead:
                    mix_outs(i + 2)

            dve.wait_ge(consts_loaded, 64)
            nc.vector.tensor_tensor(mix_w[:], mask[:], mask[:], ALU.mult).then_inc(mix_made, 1)
            dve.wait_ge(mix_made, 1)
            dve.wait_ge(ident_made, 2)
            mix_diag = mix_w[:].rearrange("p j (a c) -> p (j a) c", c=P)[:, 0:4:3, :]
            nc.vector.tensor_tensor(mix_diag, mix_diag, ident[:], ALU.add).then_inc(mix_made, 1)
            dve.wait_ge(mix_made, 2)
            nc.vector.tensor_copy(mix_s[0][:], mix_w[:]).then_inc(mix_made, 1)
            dve.wait_ge(mix_made, 3)
            lo(mix_s[1][:], mix_w[:], mix_s[0][:]).then_inc(mix_made, 1)
            dve.wait_ge(gates_exp, 2)
            nc.vector.tensor_scalar(scal[:, 4:5], scal[:, 2:3], 1.0, None, ALU.add).then_inc(gates_step, 1)
            nc.vector.tensor_tensor(scal[:, 5:6], scal[:, 3:4], scal[:, 3:4], ALU.mult).then_inc(gates_step, 1)
            dve.wait_ge(gates_step, 2)
            nc.vector.reciprocal(scal[:, 2:3], scal[:, 4:5]).then_inc(gates_step, 1)
            nc.vector.reciprocal(scal[:, 6:7], scal[:, 5:6]).then_inc(gates_step, 1)
            dve.wait_ge(gates_step, 4)
            nc.vector.tensor_scalar(branch_w[:, 0], branch_w[:, 0], scal[:, 2:3], None, ALU.mult).then_inc(gates_step, 1)
            nc.vector.tensor_scalar(d2_scale, scal[:, 6:7], -0.5, None, ALU.mult).then_inc(gates_step, 1)
            dve.wait_ge(gates_step, 5)
            nc.vector.tensor_scalar(branch_w[:, 1], branch_w[:, 0], -1.0, 1.0, ALU.mult, ALU.add).then_inc(gates_step, 1)
            dve.wait_ge(gates_step, 7)
            dve.wait_ge(weights_hi, 1)
            nc.vector.scalar_tensor_tensor(wl_s[1][:], wl_raw, 2.0, wl_s[0][:].bitcast(F32), ALU.mult,
                                           ALU.subtract).then_inc(weights_split, 1)
            dve.wait_ge(weights_split, 1)
            mix_outs(0)
            dve.wait_ge(weights_hi, 2)
            nc.vector.scalar_tensor_tensor(wg_s[1][:], wg_raw, 2.0, wg_s[0][:].bitcast(F32), ALU.mult,
                                           ALU.subtract).then_inc(weights_split, 1)
            for c in range(C):
                dve.wait_ge(wvo_hi, c + 1)
                lo(wvo_s[1][:, c], bank[HT[c]][:], wvo_s[0][:, c]).then_inc(wvo_split, 1)
            ht_los(0)
            mix_outs(1)
            body(0, True, True)
            body(1, True, True)
            with dve.Fori(2, G - 2) as i:
                body(i, True, True)
            body(G - 2, False, True)
            body(G - 1, False, False)
            lang_affinity(G - 1)
            grav_affinity(G - 1)
            degrees(G - 1)
            build_k(G - 1)
            kt_los(G - 1)
            residuals(G - 1)

        @block.tensor
        def _(pe):
            def product(dst, steps, parts=PRODUCTS):
                n, passes = 0, len(parts) * len(steps)
                for lhs, rhs in steps:
                    for a, b in parts:
                        last = nc.tensor.matmul(dst, lhs(a), rhs(b), start=(n == 0), stop=(n == passes - 1))
                        n += 1
                return last

            def mix(t):
                b, m = t // J, t % J
                steps = [(lambda s, j=j: mix_s[s][:, j, P * m:P * m + P], lambda s, j=j: x_s[s][:, J * b + j, :])
                         for j in range(J)]
                product(bank[MIX[t]][:], steps).then_inc(mix_ready, 1)

            def transpose_h(c):
                for t in range(T):
                    last = nc.tensor.transpose(bank[HT[c]][:, P * t:P * t + P], h_new[:, t, P * c:P * c + P],
                                               ident[:, 0])
                last.then_inc(ht_ready, 1)

            def projection(banks, e, w, ready):
                steps = [(lambda s, c=c: w[s][:, c, P * e:P * e + P], lambda s, c=c: h_t[s][:, c, :]) for c in range(C)]
                product(bank[banks[e]][:], steps).then_inc(ready, 1)

            def gram(banks, z, ready):
                for b in range(PAIR):
                    for j in range(J):
                        q = J * b + j
                        steps = [(lambda s, c=c: z[s][:, c, P * q:P * q + P], lambda s, c=c: z[s][:, c, N * b:N * b + N])
                                 for c in range(C)]
                        last = product(bank[banks[b]][:, N * j:N * j + N], steps, GRAM_PRODUCTS)
                    last.then_inc(ready, 1)

            def value(t):
                steps = [(lambda s, c=c: h_t[s][:, c, P * t:P * t + P], lambda s, c=c: wvo_s[s][:, c, :]) for c in range(C)]
                product(bank[VAL[t]][:], steps).then_inc(v_ready, 1)

            def rows(i):
                pe.wait_ge(r_made, i + 1)
                pe.wait_ge(gl_made, i * PAIR + 1)
                for t in range(T):
                    last = nc.tensor.transpose(bank[ROWS][:, P * t:P * t + P], r_l[:, t:t + 1].to_broadcast([P, P]),
                                               ident[:, 0])
                last.then_inc(rows_ready, 1)

            def transpose_square(dst, rows_of, b):
                for m in range(J):
                    for j in range(J):
                        last = nc.tensor.transpose(dst[:, N * m + P * j:N * m + P * j + P],
                                                   rows_of[:, J * b + j, P * m:P * m + P], ident[:, 0])
                return last

            def transpose_k(i):
                for b in range(PAIR):
                    pe.wait_ge(k_made, i * T + J * b + J)
                    transpose_square(bank[KT[b]], k_nm, b).then_inc(kt_ready, 1)

            def aggregate(i):
                pe.wait_ge(v_split, i * T + T)
                for t in range(T):
                    b, j = t // J, t % J
                    pe.wait_ge(kt_split, i * PAIR + b + 1)
                    steps = [(lambda s, m=m: k_t[s][:, J * b + m, P * j:P * j + P], lambda s, m=m: v_s[s][:, J * b + m, :])
                             for m in range(J)]
                    product(bank[AGG[t]][:], steps).then_inc(agg_ready, 1)

            def body(i, mix_ahead, norm_ahead):
                prev = later(i)
                pe.wait_ge(ht_split, i * C + C)
                if not prev:
                    pe.wait_ge(weights_split, 1)
                for e in range(C):
                    if norm_ahead:
                        pe.wait_ge(mix_out, i * T + T + e + 1)
                    elif e < 1:
                        pe.wait_ge(rows_out, i)
                    elif e < 2:
                        pe.wait_ge(gl_made, i * PAIR)
                    else:
                        pe.wait_ge(v_split, i * T - T + e + 1)
                    projection(ZL, e, wl_s, zl_ready)
                if not prev:
                    pe.wait_ge(weights_split, 2)
                for e in range(C):
                    projection(ZG, e, wg_s, zg_ready)
                pe.wait_ge(zl_split, i * C + C)
                gram(GRAM_L, zl_t, gram_l_ready)
                if prev:
                    transpose_k(i - 1)
                pe.wait_ge(zg_split, i * C + C)
                gram(GRAM_G, zg_t, gram_g_ready)
                if prev:
                    aggregate(i - 1)
                for b in range(PAIR):
                    pe.wait_ge(sl_out, i * PAIR + b + 1)
                    transpose_square(bank[SYM_L[b]], a_l, b).then_inc(sl_t_ready, 1)
                for t in range(T):
                    if prev:
                        pe.wait_ge(y_sum, i * T - T + t + 1)
                    value(t)
                    if t == 1:
                        for b in range(PAIR):
                            pe.wait_ge(sg_out, i * T + J * b + J)
                            transpose_square(bank[SYM_G[b]], a_g, b).then_inc(sg_t_ready, 1)
                        rows(i)
                if norm_ahead:
                    pe.wait_ge(h_ready, i * T + 2 * T)
                    for c in range(C):
                        if c < 2:
                            pe.wait_ge(d2_made, i * PAIR + c + 1)
                        else:
                            pe.wait_ge(v_split, i * T + c - 1)
                        transpose_h(c)
                if mix_ahead:
                    pe.wait_ge(x_split, i + 3)
                    for t in range(T):
                        if t < 1:
                            pe.wait_ge(rows_out, i + 1)
                        elif t < 2:
                            pe.wait_ge(gl_made, i * PAIR + PAIR)
                        else:
                            pe.wait_ge(v_split, i * T + t + 1)
                        mix(t)

            pe.wait_ge(mix_made, 4)
            pe.wait_ge(x_split, 1)
            for t in range(T):
                mix(t)
            pe.wait_ge(vo_loaded, 32)
            for c in range(C):
                for v in range(C):
                    last = nc.tensor.matmul(bank[HT[c]][:], wv_raw[:, v, P * c:P * c + P], wo_raw[:, v, :],
                                            start=(v == 0), stop=(v == C - 1))
                last.then_inc(wvo_ready, 1)
            pe.wait_ge(h_ready, T)
            for c in range(C):
                pe.wait_ge(wvo_split, c + 1)
                transpose_h(c)
            pe.wait_ge(x_split, 2)
            for t in range(T):
                pe.wait_ge(mix_out, t + 1)
                mix(t)
            body(0, True, True)
            body(1, True, True)
            with pe.Fori(2, G - 2) as i:
                body(i, True, True)
            body(G - 2, False, True)
            body(G - 1, False, False)
            pe.wait_ge(v_split, G * T)
            transpose_k(G - 1)
            aggregate(G - 1)

    return nc


def kernel(x, adj, L0_gnn_bias, L1_gnn_W_lang, L1_gnn_W_grav, L1_gnn_W_V, L1_gnn_W_O, L1_gnn_gate_logit,
           L1_gnn_log_sigma):
    import numpy as np
    import concourse.bacc as bacc
    from concourse.bass_utils import run_bass_kernel_spmd

    arrays = {
        "x": np.ascontiguousarray(x),
        "adj": np.ascontiguousarray(adj),
        "bias": np.ascontiguousarray(L0_gnn_bias).reshape(1, -1),
        "w_lang_t": np.ascontiguousarray(np.asarray(L1_gnn_W_lang).T),
        "w_grav_t": np.ascontiguousarray(np.asarray(L1_gnn_W_grav).T),
        "w_v": np.ascontiguousarray(L1_gnn_W_V),
        "w_o_t": np.ascontiguousarray(np.asarray(L1_gnn_W_O).T),
        "gate": np.ascontiguousarray(L1_gnn_gate_logit).reshape(1, 1),
        "log_sigma": np.ascontiguousarray(L1_gnn_log_sigma).reshape(1, 1),
    }
    nc = bacc.Bacc("TRN2", target_bir_lowering=False, num_devices=1)
    args = [nc.dram_tensor(name, a.shape, F32, kind="ExternalInput").ap() for name, a in arrays.items()]
    out = nc.dram_tensor("out", arrays["x"].shape, F32, kind="ExternalOutput").ap()
    bass_adj_resnorm_kernel(nc, *args, out)
    return run_bass_kernel_spmd(nc, [arrays], core_ids=[0]).results[0]["out"]
```

```python
from contextlib import ExitStack

import concourse.bass as bass
from concourse import mybir

F32 = mybir.dt.float32
F32R = mybir.dt.float32r
ALU = mybir.AluOpType
ACT = mybir.ActivationFunctionType
AX_X = mybir.AxisListType.X

P = 128
LN_EPS = 1e-5
EPS = 1e-8

PRODUCTS = ((0, 0), (0, 1), (1, 0))

GRAM_PRODUCTS = ((0, 0), (0, 1))


def bass_adj_resnorm_kernel(nc, x, adj, bias, w_lang_t, w_grav_t, w_v, w_o_t, gate, log_sigma, out):
    B, N, D = x.shape
    PAIR = 2
    J = N // P
    T = PAIR * J
    C = D // P
    TOK = PAIR * N
    G = B // PAIR
    assert N == 2 * P and D == 512 and TOK == 512 and T == 4 and C == 4 and G >= 5

    x_pairs = x.rearrange("b n f -> (b n) f").rearrange("(g t p) f -> g p t f", t=T, p=P)
    out_pairs = out.rearrange("b n f -> (b n) f").rearrange("(g t p) f -> g p t f", t=T, p=P)

    with ExitStack() as ctx:
        def sb(name, shape, dt=F32):
            return ctx.enter_context(nc.sbuf_tensor(name, shape, dt))

        def sem(name):
            return ctx.enter_context(nc.semaphore(name))

        def split(name, shape):
            return [sb(name + "_hi", shape, F32R), sb(name + "_lo", shape, F32R)]

        x_raw = sb("x_raw", [P, T, D])
        x_s = split("x", [P, T, D])
        mixed = sb("mixed", [P, T, D])
        h_new = sb("h_new", [P, T, D])
        h_res = sb("h_res", [P, T, D])
        h_t = split("h_t", [P, C, TOK])
        zl_t = split("zl_t", [P, C, TOK])
        zg_t = split("zg_t", [P, C, TOK])
        v_s = split("v", [P, T, D])
        y = sb("y", [P, T, D])
        wl_s = split("wl", [P, C, D])
        wg_s = split("wg", [P, C, D])
        wvo_s = split("wvo", [P, C, D])
        mix_s = split("mix", [P, J, N])
        mix_w = sb("mix_w", [P, J, N])
        mask = sb("mask", [P, J, N])
        bias_b = sb("bias_b", [P, D])
        ident = sb("ident", [P, J, P])
        aff = sb("aff", [P, 2, T, N])
        a_l, a_g = aff[:, 0], aff[:, 1]
        k_nm = sb("k_nm", [P, T, N])
        k_t = split("k_t", [P, T, N])
        row_r = sb("row_r", [P, T * P])
        diag = sb("diag", [P, 2 * PAIR, J, P])
        norm2 = sb("norm2", [P, 2, T])
        guarded = sb("guarded", [P, T])
        r_l = sb("r_l", [P, T])
        deg = sb("deg", [P, 2, T])
        deg_max = sb("deg_max", [P, 2, T])
        deg_inv = sb("deg_inv", [P, 2, T])
        coef = sb("coef", [P, 2, T])
        branch_w = sb("branch_w", [P, 2, T])
        stats1 = sb("stats1", [P, T, 6])
        mv1 = sb("mv1", [P, T, 2])
        rstd1 = sb("rstd1", [P, 4, T])
        stats2 = sb("stats2", [P, T, 6])
        mv2 = sb("mv2", [P, T, 2])
        rstd2 = sb("rstd2", [P, 4, T])
        minus_half = sb("minus_half", [P, T])
        mix_lo_max = sb("mix_lo_max", [P, 2])
        scal = sb("scal", [P, 8])
        d2_scale = scal[:, 7:8]

        bank = [ctx.enter_context(nc.psum_tensor(f"bank{i}", [P, 512], F32)) for i in range(8)]

        wl_raw, wg_raw, wv_raw = mixed[:], h_res[:], y[:]
        wo_raw = aff[:].rearrange("p a t n -> p (a t n)").rearrange("p (c e) -> p c e", c=C)

        ZL, ZG, GRAM_L, KT, GRAM_G = (0, 1, 2, 3), (4, 5, 6, 7), (0, 1), (2, 3), (4, 5)
        AGG, SYM_L, VAL, SYM_G, ROWS = (6, 7, 2, 3), (0, 1), (6, 7, 2, 3), (4, 5), 0
        HT, MIX = (4, 5, 6, 7), (0, 1, 2, 3)

        adj_loaded = sem("adj_loaded")
        consts_loaded = sem("consts_loaded")
        wl_loaded = sem("wl_loaded")
        wg_loaded = sem("wg_loaded")
        vo_loaded = sem("vo_loaded")
        ident_made = sem("ident_made")
        gates_exp = sem("gates_exp")
        gates_step = sem("gates_step")
        mix_made = sem("mix_made")
        weights_hi = sem("weights_hi")
        weights_split = sem("weights_split")
        wvo_ready = sem("wvo_ready")
        wvo_hi = sem("wvo_hi")
        wvo_split = sem("wvo_split")
        mask_made = sem("mask_made")
        mix_lo_top = sem("mix_lo_top")
        mix_lo_known = sem("mix_lo_known")

        first_loaded = [sem(f"first_loaded{b}") for b in range(PAIR)]
        first_hi = sem("first_hi")
        first_split = sem("first_split")
        x_loaded = sem("x_loaded")
        x_hi_made = sem("x_hi_made")
        x_split = sem("x_split")
        mix_ready = sem("mix_ready")
        mix_out = sem("mix_out")
        stats1_made = sem("stats1_made")
        mean1_made = sem("mean1_made")
        rstd1_step = sem("rstd1_step")
        h_ready = sem("h_ready")
        h_saved = sem("h_saved")
        ht_ready = sem("ht_ready")
        ht_hi = sem("ht_hi")
        ht_split = sem("ht_split")
        zl_ready = sem("zl_ready")
        zl_hi = sem("zl_hi")
        zl_split = sem("zl_split")
        zg_ready = sem("zg_ready")
        zg_hi = sem("zg_hi")
        zg_split = sem("zg_split")
        gram_l_ready = sem("gram_l_ready")
        gram_g_ready = sem("gram_g_ready")
        diag_cut = sem("diag_cut")
        diag_l = sem("diag_l")
        diag_g = sem("diag_g")
        r_guarded = sem("r_guarded")
        r_made = sem("r_made")
        sl_out = sem("sl_out")
        sg_out = sem("sg_out")
        sl_t_ready = sem("sl_t_ready")
        sg_t_ready = sem("sg_t_ready")
        rows_ready = sem("rows_ready")
        rows_out = sem("rows_out")
        gl_made = sem("gl_made")
        d2_made = sem("d2_made")
        al_masked = sem("al_masked")
        exp_made = sem("exp_made")
        al_made = sem("al_made")
        ag_made = sem("ag_made")
        coef_step = sem("coef_step")
        al_scaled = sem("al_scaled")
        k_made = sem("k_made")
        kt_ready = sem("kt_ready")
        kt_hi = sem("kt_hi")
        kt_split = sem("kt_split")
        v_ready = sem("v_ready")
        v_hi = sem("v_hi")
        v_split = sem("v_split")
        agg_ready = sem("agg_ready")
        y_sum = sem("y_sum")
        stats2_made = sem("stats2_made")
        mean2_made = sem("mean2_made")
        rstd2_step = sem("rstd2_step")
        y_ready = sem("y_ready")
        stored = sem("stored")

        def later(i):
            return not (isinstance(i, int) and i <= 0)

        block = ctx.enter_context(nc.Block())

        @block.sync
        def _(sp):
            def load_x(k):
                if isinstance(k, int) and k == 1:
                    sp.wait_ge(first_split, PAIR)
                else:
                    sp.wait_ge(x_split, k - 1)
                sp.dma_start(x_raw[:], x_pairs[bass.ds(k, 1)].rearrange("g p t f -> p (g t) f")).then_inc(x_loaded, 16)

            def store(k):
                sp.wait_ge(y_ready, k * T + T)
                sp.dma_start(out_pairs[bass.ds(k, 1)].rearrange("g p t f -> p (g t) f"), y[:]).then_inc(stored, 16)

            sp.dma_start(mask[:], adj.rearrange("(j p) m -> p j m", p=P)).then_inc(adj_loaded, 16)
            for b in range(PAIR):
                half = slice(J * b, J * b + J)
                sp.dma_start(x_raw[:, half], x_pairs[0][:, half]).then_inc(first_loaded[b], 16)
            sp.dma_start(bias_b[:], bias.broadcast_to([P, D])).then_inc(consts_loaded, 16)
            sp.dma_start(scal[:, 0:1], gate.broadcast_to([P, 1])).then_inc(consts_loaded, 16)
            sp.dma_start(scal[:, 1:2], log_sigma.broadcast_to([P, 1])).then_inc(consts_loaded, 16)
            sp.dma_start(wl_raw, w_lang_t.rearrange("(c p) e -> p c e", p=P)).then_inc(wl_loaded, 16)
            sp.dma_start(wv_raw, w_v.rearrange("(c p) e -> p c e", p=P)).then_inc(vo_loaded, 16)
            sp.dma_start(wo_raw, w_o_t.rearrange("(c p) e -> p c e", p=P)).then_inc(vo_loaded, 16)
            sp.dma_start(wg_raw, w_grav_t.rearrange("(c p) e -> p c e", p=P)).then_inc(wg_loaded, 16)
            load_x(1)
            load_x(2)
            load_x(3)
            with sp.Fori(1, G - 3) as i:
                store(i - 1)
                load_x(i + 3)
            for k in range(G - 4, G - 1):
                store(k)
            for t in range(T):
                sp.wait_ge(y_ready, (G - 1) * T + t + 1)
                sp.dma_start(out_pairs[G - 1][:, t], y[:, t]).then_inc(stored, 16)
            sp.wait_ge(stored, 16 * (G - 1 + T))


        @block.gpsimd
        def _(pool):
            def split_x(k):
                pool.wait_ge(x_hi_made, k)
                nc.gpsimd.tensor_tensor(x_s[1][:], x_raw[:], x_s[0][:].bitcast(F32), ALU.subtract).then_inc(x_split, 1)

            def norm_factors(k, mv, f, mean_made, step):
                pool.wait_ge(mean_made, k * T + T)
                pool.nop(nofuse=True)
                nc.gpsimd.tensor_scalar(f[:, 0, :], mv[:, :, 1], LN_EPS, None, ALU.add).then_inc(step, 1)
                nc.gpsimd.tensor_scalar(f[:, 1, :], mv[:, :, 0], -1.0, None, ALU.mult).then_inc(step, 1)
                pool.wait_ge(step, k * 4 + 1)
                nc.gpsimd.tensor_tensor(f[:, 2, :], f[:, 0, :], minus_half[:], ALU.pow).then_inc(step, 1)
                pool.wait_ge(step, k * 4 + 3)
                nc.gpsimd.tensor_tensor(f[:, 3, :], f[:, 1, :], f[:, 2, :], ALU.mult).then_inc(step, 1)

            def last_norm_factors(t):
                done = (G - 1 + t) * 4
                pool.wait_ge(mean2_made, (G - 1) * T + t + 1)
                nc.gpsimd.tensor_scalar(rstd2[:, 0, t:t + 1], mv2[:, t, 1:2], LN_EPS, None, ALU.add).then_inc(rstd2_step, 1)
                nc.gpsimd.tensor_scalar(rstd2[:, 1, t:t + 1], mv2[:, t, 0:1], -1.0, None, ALU.mult).then_inc(rstd2_step, 1)
                pool.wait_ge(rstd2_step, done + 1)
                nc.gpsimd.tensor_tensor(rstd2[:, 2, t:t + 1], rstd2[:, 0, t:t + 1], minus_half[:, 0:1],
                                        ALU.pow).then_inc(rstd2_step, 1)
                pool.wait_ge(rstd2_step, done + 3)
                nc.gpsimd.tensor_tensor(rstd2[:, 3, t:t + 1], rstd2[:, 1, t:t + 1], rstd2[:, 2, t:t + 1],
                                        ALU.mult).then_inc(rstd2_step, 1)

            def lang_norms(i):
                pool.wait_ge(diag_l, i * PAIR + PAIR)
                pool.nop(nofuse=True)
                nc.gpsimd.tensor_scalar(guarded[:], norm2[:, 0, :], EPS * EPS, None, ALU.max).then_inc(r_guarded, 1)
                pool.wait_ge(r_guarded, i + 1)
                if later(i):
                    pool.wait_ge(rows_ready, i)
                    pool.wait_ge(al_made, i * T)
                nc.gpsimd.tensor_tensor(r_l[:], guarded[:], minus_half[:], ALU.pow).then_inc(r_made, 1)

            def save_h(i):
                if not later(i):
                    pool.wait_ge(weights_split, 2)
                for t in range(T):
                    if later(i):
                        pool.wait_ge(y_sum, i * T - T + t + 1)
                        pool.nop(nofuse=True)
                    nc.gpsimd.tensor_copy(h_res[:, t], h_new[:, t]).then_inc(h_saved, 1)

            def body(i, mix_ahead, norm_ahead):
                if norm_ahead:
                    norm_factors(i + 1, mv1, rstd1, mean1_made, rstd1_step)
                if mix_ahead:
                    split_x(i + 2)
                lang_norms(i)
                save_h(i)
                if later(i):
                    norm_factors(i - 1, mv2, rstd2, mean2_made, rstd2_step)

            nc.gpsimd.memset(minus_half[:], -0.5)
            nc.gpsimd.memset(branch_w[:], 1.0)
            nc.gpsimd.memset(ident[:], 0.0).then_inc(ident_made, 1)
            pool.wait_ge(ident_made, 1)
            nc.gpsimd.affine_select(out=ident[:], in_=ident[:], compare_op=ALU.not_equal, fill=1.0, base=0,
                                    pattern=[[0, J], [-1, P]], channel_multiplier=1).then_inc(ident_made, 1)
            pool.wait_ge(mix_made, 1)
            nc.gpsimd.affine_select(out=mask[:], in_=mask[:], compare_op=ALU.not_equal, fill=0.0, base=0,
                                    pattern=[[P, J], [-1, N]], channel_multiplier=1).then_inc(mask_made, 1)
            pool.wait_ge(mix_lo_top, 1)
            nc.gpsimd.partition_all_reduce(mix_lo_max[:, 1:2], mix_lo_max[:, 0:1], P,
                                           bass.bass_isa.ReduceOp.max).then_inc(mix_lo_known, 1)
            norm_factors(0, mv1, rstd1, mean1_made, rstd1_step)
            split_x(1)
            body(0, True, True)
            body(1, True, True)
            with pool.Fori(2, G - 2) as i:
                body(i, True, True)
            body(G - 2, False, True)
            body(G - 1, False, False)
            for t in range(T):
                last_norm_factors(t)

        @block.scalar
        def _(act):
            def hi(dst, src):
                return nc.scalar.activation(dst, src, ACT.Identity)

            def x_his(k):
                act.wait_ge(x_loaded, k * 16)
                act.wait_ge(mix_ready, k * T)
                hi(x_s[0][:], x_raw[:]).then_inc(x_hi_made, 1)

            def hi_of_double(dst, src):
                return nc.scalar.activation(dst, src, ACT.Identity, scale=0.5)

            def norm1(k):
                act.wait_ge(rstd1_step, k * 4 + 4)
                if later(k):
                    act.wait_ge(ht_ready, k * C)
                for t in range(T):
                    if later(k):
                        act.wait_ge(h_saved, k * T - T + t + 1)
                    nc.scalar.activation(h_new[:, t], mixed[:, t], ACT.Identity, bias=rstd1[:, 3, t:t + 1],
                                         scale=rstd1[:, 2, t:t + 1]).then_inc(h_ready, 1)

            def norm2_out(k):
                act.wait_ge(rstd2_step, k * 4 + 4)
                for t in range(T):
                    nc.scalar.activation(y[:, t], y[:, t], ACT.Identity, bias=rstd2[:, 3, t:t + 1],
                                         scale=rstd2[:, 2, t:t + 1]).then_inc(y_ready, 1)

            def ht_his(k):
                if later(k):
                    act.wait_ge(v_ready, k * T)
                for c in range(C):
                    act.wait_ge(ht_ready, k * C + c + 1)
                    hi(h_t[0][:, c], bank[HT[c]][:]).then_inc(ht_hi, 1)

            def val_his(i, ts):
                if later(i):
                    act.wait_ge(agg_ready, i * T)
                for t in ts:
                    act.wait_ge(v_ready, i * T + t + 1)
                    hi(v_s[0][:, t], bank[VAL[t]][:]).then_inc(v_hi, 1)

            def exps(i):
                for b in range(PAIR):
                    act.wait_ge(d2_made, i * PAIR + b + 1)
                    nc.scalar.activation(a_g[:, J * b:J * b + J], a_g[:, J * b:J * b + J], ACT.Exp,
                                         scale=d2_scale).then_inc(exp_made, 1)

            def scale_lang(i):
                act.wait_ge(coef_step, i * 3 + 3)
                for t in range(T):
                    nc.scalar.activation(a_l[:, t], a_l[:, t], ACT.Identity,
                                         scale=coef[:, 0, t:t + 1]).then_inc(al_scaled, 1)

            def kt_his(i, banks=KT):
                if later(i - 1):
                    act.wait_ge(agg_ready, i * T)
                for b in range(PAIR):
                    act.wait_ge(kt_ready, i * PAIR + b + 1)
                    hi(k_t[0][:, J * b:J * b + J], bank[banks[b]][:]).then_inc(kt_hi, 1)

            def body(i, mix_ahead, norm_ahead):
                prev = later(i)
                if prev:
                    act.wait_ge(gram_l_ready, i * PAIR)
                for e in range(C):
                    act.wait_ge(zl_ready, i * C + e + 1)
                    hi_of_double(zl_t[0][:, e], bank[ZL[e]][:]).then_inc(zl_hi, 1)
                    if prev and e == 0:
                        exps(i - 1)
                    if mix_ahead and e == 2:
                        x_his(i + 2)
                if prev:
                    act.wait_ge(gram_g_ready, i * PAIR)
                for e in range(C):
                    act.wait_ge(zg_ready, i * C + e + 1)
                    hi_of_double(zg_t[0][:, e], bank[ZG[e]][:]).then_inc(zg_hi, 1)
                    if prev and e == 1:
                        scale_lang(i - 1)
                if prev:
                    act.wait_ge(k_made, i * T)
                for b in range(PAIR):
                    act.wait_ge(diag_l, i * PAIR + b + 1)
                    nc.scalar.copy(a_l[:, J * b:J * b + J].rearrange("p j n -> p (j n)"),
                                   bank[GRAM_L[b]][:]).then_inc(sl_out, 1)
                if prev:
                    kt_his(i - 1)
                for t in range(T):
                    act.wait_ge(diag_g, i * PAIR + t // J + 1)
                    nc.scalar.activation(a_g[:, t], bank[GRAM_G[t // J]][:, N * (t % J):N * (t % J) + N],
                                         ACT.Identity, bias=norm2[:, 1, t:t + 1], scale=-1.0).then_inc(sg_out, 1)
                def row_out():
                    if prev:
                        act.wait_ge(al_made, i * T)
                    act.wait_ge(rows_ready, i + 1)
                    nc.scalar.activation(row_r[:], bank[ROWS][:], ACT.Copy, scale=0.5).then_inc(rows_out, 1)

                if norm_ahead:
                    val_his(i, (0, 1))
                    norm1(i + 1)
                    row_out()
                    val_his(i, (2, 3))
                    ht_his(i + 1)
                    if prev:
                        norm2_out(i - 1)
                else:
                    val_his(i, (0,))
                    row_out()
                    exps(i)
                    val_his(i, (1,))
                    norm2_out(i - 1)
                    scale_lang(i)
                    val_his(i, (2, 3))
                    kt_his(i, SYM_G)

            for b in range(PAIR):
                act.wait_ge(first_loaded[b], 16)
                hi(x_s[0][:, J * b:J * b + J], x_raw[:, J * b:J * b + J]).then_inc(first_hi, 1)
            act.wait_ge(consts_loaded, 48)
            nc.scalar.activation(scal[:, 2:3], scal[:, 0:1], ACT.Exp, scale=-1.0).then_inc(gates_exp, 1)
            nc.scalar.activation(scal[:, 3:4], scal[:, 1:2], ACT.Exp).then_inc(gates_exp, 1)
            act.wait_ge(wl_loaded, 16)
            nc.scalar.activation(wl_s[0][:], wl_raw, ACT.Identity, scale=2.0).then_inc(weights_hi, 1)
            act.wait_ge(wg_loaded, 16)
            nc.scalar.activation(wg_s[0][:], wg_raw, ACT.Identity, scale=2.0).then_inc(weights_hi, 1)
            norm1(0)
            x_his(1)
            for c in range(C):
                act.wait_ge(wvo_ready, c + 1)
                hi(wvo_s[0][:, c], bank[HT[c]][:]).then_inc(wvo_hi, 1)
            ht_his(0)
            body(0, True, True)
            body(1, True, True)
            with act.Fori(2, G - 2) as i:
                body(i, True, True)
            body(G - 2, False, True)
            body(G - 1, False, False)
            for t in range(T):
                act.wait_ge(rstd2_step, (G + t) * 4)
                nc.scalar.activation(y[:, t], y[:, t], ACT.Identity, bias=rstd2[:, 3, t:t + 1],
                                     scale=rstd2[:, 2, t:t + 1]).then_inc(y_ready, 1)

        @block.vector
        def _(dve):
            def lo(dst, src, hi_part):
                return nc.vector.tensor_tensor(dst, src, hi_part.bitcast(F32), ALU.subtract)

            def layer_stats(k, t, src, stats, mv, summed, stats_made, mean_made):
                dve.wait_ge(summed, k * T + t + 1)
                nc.vector.bn_stats(stats[:, t, :], src[:, t]).then_inc(stats_made, 1)
                dve.wait_ge(stats_made, k * T + t + 1)
                dve.nop(nofuse=True)
                nc.vector.bn_aggr(mv[:, t, :], stats[:, t, :]).then_inc(mean_made, 1)

            def mix_outs(k):
                for t in range(T):
                    dve.wait_ge(mix_ready, k * T + t + 1)
                    if later(k):
                        dve.wait_ge(h_ready, (k - 1) * T + t + 1)
                    nc.vector.tensor_tensor(mixed[:, t], bank[MIX[t]][:], bias_b[:], ALU.add).then_inc(mix_out, 1)
                    layer_stats(k, t, mixed, stats1, mv1, mix_out, stats1_made, mean1_made)

            def ht_los(k):
                for c in range(C):
                    dve.wait_ge(ht_hi, k * C + c + 1)
                    lo(h_t[1][:, c], bank[HT[c]][:], h_t[0][:, c]).then_inc(ht_split, 1)

            def lo_twice(dst, double, hi_part):
                return nc.vector.scalar_tensor_tensor(dst, hi_part.bitcast(F32), -2.0, double, ALU.mult, ALU.add)

            def symmetrize(i, part, banks, ready, done):
                for b in range(PAIR):
                    dve.wait_ge(ready, i * PAIR + b + 1)
                    flat = part[:, J * b:J * b + J].rearrange("p j n -> p (j n)")
                    nc.vector.tensor_tensor(flat, bank[banks[b]][:], flat, ALU.add).then_inc(done, 1)

            def mask_lang(i):
                for b in range(PAIR):
                    dve.wait_ge(gl_made, i * PAIR + b + 1)
                    nc.vector.scalar_tensor_tensor(a_l[:, J * b:J * b + J], a_l[:, J * b:J * b + J], 0.0, mask[:],
                                                   ALU.max, ALU.mult).then_inc(al_masked, 1)

            def lang_affinity(i):
                dve.wait_ge(rows_out, i + 1)
                for t in range(T):
                    dve.wait_ge(al_masked, i * PAIR + t // J + 1)
                    nc.vector.scalar_tensor_tensor(a_l[:, t], a_l[:, t], r_l[:, t:t + 1],
                                                   row_r[:, N * (t // J):N * (t // J) + N],
                                                   ALU.mult, ALU.mult, accum_out=deg[:, 0, t:t + 1]).then_inc(al_made, 1)

            def grav_affinity(i):
                for t in range(T):
                    dve.wait_ge(exp_made, i * PAIR + t // J + 1)
                    nc.vector.scalar_tensor_tensor(a_g[:, t], a_g[:, t], 1.0, mask[:, t % J],
                                                   ALU.min, ALU.mult, accum_out=deg[:, 1, t:t + 1]).then_inc(ag_made, 1)

            def degrees(i):
                dve.wait_ge(al_made, i * T + T)
                dve.wait_ge(ag_made, i * T + T)
                nc.vector.tensor_scalar(deg_max[:], deg[:], EPS, None, ALU.max).then_inc(coef_step, 1)
                dve.wait_ge(coef_step, i * 3 + 1)
                nc.vector.reciprocal(deg_inv[:], deg_max[:]).then_inc(coef_step, 1)
                dve.wait_ge(coef_step, i * 3 + 2)
                nc.vector.tensor_tensor(coef[:], deg_inv[:], branch_w[:], ALU.mult).then_inc(coef_step, 1)

            def build_k(i):
                if later(i - 1):
                    dve.wait_ge(kt_ready, i * PAIR)
                dve.wait_ge(coef_step, i * 3 + 3)
                for t in range(T):
                    dve.wait_ge(al_scaled, i * T + t + 1)
                    nc.vector.scalar_tensor_tensor(k_nm[:, t], a_g[:, t], coef[:, 1, t:t + 1], a_l[:, t],
                                                   ALU.mult, ALU.add).then_inc(k_made, 1)

            def diagonals(i, which, banks, ready, done):
                if later(i):
                    dve.wait_ge(done, i * PAIR)
                for b in range(PAIR):
                    dve.wait_ge(ready, i * PAIR + b + 1)
                    blocks = bank[banks[b]][:].rearrange("p (a c) -> p a c", c=P)[:, 0:4:3, :]
                    nc.vector.tensor_tensor(diag[:, which * PAIR + b], blocks, ident[:], ALU.mult).then_inc(diag_cut, 1)
                    dve.wait_ge(diag_cut, i * 2 * PAIR + which * PAIR + b + 1)
                    nc.vector.reduce_sum(norm2[:, which, J * b:J * b + J], diag[:, which * PAIR + b], axis=AX_X).then_inc(done, 1)

            def kt_los(i, banks=KT):
                for b in range(PAIR):
                    dve.wait_ge(kt_hi, i * PAIR + b + 1)
                    lo(k_t[1][:, J * b:J * b + J], bank[banks[b]][:].rearrange("p (j n) -> p j n", j=J),
                       k_t[0][:, J * b:J * b + J]).then_inc(kt_split, 1)

            def residuals(i):
                if later(i):
                    dve.wait_ge(stored, i * 16)
                for t in range(T):
                    dve.wait_ge(h_saved, i * T + t + 1)
                    dve.wait_ge(agg_ready, i * T + t + 1)
                    nc.vector.tensor_tensor(y[:, t], bank[AGG[t]][:], h_res[:, t], ALU.add).then_inc(y_sum, 1)
                    layer_stats(i, t, y, stats2, mv2, y_sum, stats2_made, mean2_made)

            def val_los(i, ts):
                for t in ts:
                    dve.wait_ge(v_hi, i * T + t + 1)
                    lo(v_s[1][:, t], bank[VAL[t]][:], v_s[0][:, t]).then_inc(v_split, 1)

            def body(i, mix_ahead, norm_ahead):
                prev = later(i)
                for e in range(C):
                    dve.wait_ge(zl_hi, i * C + e + 1)
                    lo_twice(zl_t[1][:, e], bank[ZL[e]][:], zl_t[0][:, e]).then_inc(zl_split, 1)
                    if prev and e == 0:
                        lang_affinity(i - 1)
                    if prev and e == 1:
                        grav_affinity(i - 1)
                        degrees(i - 1)
                for e in range(C):
                    dve.wait_ge(zg_hi, i * C + e + 1)
                    lo_twice(zg_t[1][:, e], bank[ZG[e]][:], zg_t[0][:, e]).then_inc(zg_split, 1)
                    if prev and e == 1:
                        build_k(i - 1)
                if prev:
                    dve.wait_ge(r_guarded, i)
                diagonals(i, 0, GRAM_L, gram_l_ready, diag_l)
                if prev:
                    kt_los(i - 1)
                    dve.wait_ge(sg_out, i * T)
                diagonals(i, 1, GRAM_G, gram_g_ready, diag_g)
                if prev:
                    residuals(i - 1)
                symmetrize(i, a_l, SYM_L, sl_t_ready, gl_made)
                if norm_ahead:
                    val_los(i, (0, 1))
                    symmetrize(i, a_g, SYM_G, sg_t_ready, d2_made)
                    mask_lang(i)
                    val_los(i, (2, 3))
                else:
                    symmetrize(i, a_g, SYM_G, sg_t_ready, d2_made)
                    mask_lang(i)
                    val_los(i, (0,))
                    lang_affinity(i)
                    grav_affinity(i)
                    degrees(i)
                    val_los(i, (1,))
                    build_k(i)
                    val_los(i, (2, 3))
                    kt_los(i, SYM_G)
                if norm_ahead:
                    ht_los(i + 1)
                if mix_ahead:
                    mix_outs(i + 2)

            dve.wait_ge(adj_loaded, 16)
            nc.vector.tensor_tensor(mix_w[:], mask[:], mask[:], ALU.mult).then_inc(mix_made, 1)
            dve.wait_ge(mix_made, 1)
            dve.wait_ge(ident_made, 2)
            mix_diag = mix_w[:].rearrange("p j (a c) -> p (j a) c", c=P)[:, 0:4:3, :]
            nc.vector.tensor_tensor(mix_diag, mix_diag, ident[:], ALU.add).then_inc(mix_made, 1)
            dve.wait_ge(mix_made, 2)
            nc.vector.tensor_copy(mix_s[0][:], mix_w[:]).then_inc(mix_made, 1)
            dve.wait_ge(mix_made, 3)
            lo(mix_s[1][:], mix_w[:], mix_s[0][:]).then_inc(mix_made, 1)
            for b in range(PAIR):
                half = slice(J * b, J * b + J)
                dve.wait_ge(first_hi, b + 1)
                lo(x_s[1][:, half], x_raw[:, half], x_s[0][:, half]).then_inc(first_split, 1)
            dve.wait_ge(mix_made, 4)
            nc.vector.tensor_reduce(mix_lo_max[:, 0:1], mix_s[1][:].bitcast(F32), op=ALU.max, axis=mybir.AxisListType.XY,
                                    apply_absolute_value=True).then_inc(mix_lo_top, 1)
            dve.wait_ge(gates_exp, 2)
            nc.vector.tensor_scalar(scal[:, 4:5], scal[:, 2:3], 1.0, None, ALU.add).then_inc(gates_step, 1)
            nc.vector.tensor_tensor(scal[:, 5:6], scal[:, 3:4], scal[:, 3:4], ALU.mult).then_inc(gates_step, 1)
            dve.wait_ge(gates_step, 2)
            nc.vector.reciprocal(scal[:, 2:3], scal[:, 4:5]).then_inc(gates_step, 1)
            nc.vector.reciprocal(scal[:, 6:7], scal[:, 5:6]).then_inc(gates_step, 1)
            dve.wait_ge(gates_step, 4)
            nc.vector.tensor_scalar(branch_w[:, 0], branch_w[:, 0], scal[:, 2:3], None, ALU.mult).then_inc(gates_step, 1)
            nc.vector.tensor_scalar(d2_scale, scal[:, 6:7], -0.5, None, ALU.mult).then_inc(gates_step, 1)
            dve.wait_ge(gates_step, 5)
            nc.vector.tensor_scalar(branch_w[:, 1], branch_w[:, 0], -1.0, 1.0, ALU.mult, ALU.add).then_inc(gates_step, 1)
            dve.wait_ge(gates_step, 7)
            dve.wait_ge(weights_hi, 1)
            nc.vector.scalar_tensor_tensor(wl_s[1][:], wl_raw, 2.0, wl_s[0][:].bitcast(F32), ALU.mult,
                                           ALU.subtract).then_inc(weights_split, 1)
            dve.wait_ge(weights_split, 1)
            dve.wait_ge(consts_loaded, 48)
            mix_outs(0)
            dve.wait_ge(weights_hi, 2)
            nc.vector.scalar_tensor_tensor(wg_s[1][:], wg_raw, 2.0, wg_s[0][:].bitcast(F32), ALU.mult,
                                           ALU.subtract).then_inc(weights_split, 1)
            for c in range(C):
                dve.wait_ge(wvo_hi, c + 1)
                lo(wvo_s[1][:, c], bank[HT[c]][:], wvo_s[0][:, c]).then_inc(wvo_split, 1)
            ht_los(0)
            mix_outs(1)
            body(0, True, True)
            body(1, True, True)
            with dve.Fori(2, G - 2) as i:
                body(i, True, True)
            body(G - 2, False, True)
            body(G - 1, False, False)
            residuals(G - 1)

        @block.tensor
        def _(pe):
            def product(dst, steps, parts=PRODUCTS):
                n, passes = 0, len(parts) * len(steps)
                for lhs, rhs in steps:
                    for a, b in parts:
                        last = nc.tensor.matmul(dst, lhs(a), rhs(b), start=(n == 0), stop=(n == passes - 1))
                        n += 1
                return last

            def mix_pass(t, w_part, x_part, j, start=False, stop=False):
                m = t % J
                return nc.tensor.matmul(bank[MIX[t]][:], mix_s[w_part][:, j, P * m:P * m + P],
                                        x_s[x_part][:, t - m + j, :], start=start, stop=stop)

            def mix_begin(t):
                mix_pass(t, 0, 0, 0, start=True)
                mix_pass(t, 0, 1, 0)
                mix_pass(t, 0, 0, 1)

            def mix_lo_passes():
                for t in range(T):
                    for j in range(J):
                        mix_pass(t, 1, 0, j)

            def mix_end():
                for t in range(T):
                    mix_pass(t, 0, 1, 1, stop=True).then_inc(mix_ready, 1)

            def transpose_h(c):
                for t in range(T):
                    last = nc.tensor.transpose(bank[HT[c]][:, P * t:P * t + P], h_new[:, t, P * c:P * c + P],
                                               ident[:, 0])
                last.then_inc(ht_ready, 1)

            def projection(banks, e, w, ready):
                steps = [(lambda s, c=c: w[s][:, c, P * e:P * e + P], lambda s, c=c: h_t[s][:, c, :]) for c in range(C)]
                product(bank[banks[e]][:], steps).then_inc(ready, 1)

            def last_lang():
                for c in range(C):
                    pe.wait_ge(ht_split, (G - 1) * C + c + 1)
                    for e in range(C):
                        if c == 0 and e == 0:
                            pe.wait_ge(rows_out, G - 1)
                        elif c == 0 and e == 1:
                            pe.wait_ge(gl_made, (G - 1) * PAIR)
                        elif c == 0:
                            pe.wait_ge(v_split, (G - 2) * T + e + 1)
                        for n, (a, b) in enumerate(PRODUCTS):
                            last = nc.tensor.matmul(bank[ZL[e]][:], wl_s[a][:, c, P * e:P * e + P], h_t[b][:, c, :],
                                                    start=(c == 0 and n == 0),
                                                    stop=(c == C - 1 and n == len(PRODUCTS) - 1))
                        if c == C - 1:
                            last.then_inc(zl_ready, 1)

            def gram(banks, z, ready):
                for b in range(PAIR):
                    for j in range(J):
                        q = J * b + j
                        steps = [(lambda s, c=c: z[s][:, c, P * q:P * q + P], lambda s, c=c: z[s][:, c, N * b:N * b + N])
                                 for c in range(C)]
                        last = product(bank[banks[b]][:, N * j:N * j + N], steps, GRAM_PRODUCTS)
                    last.then_inc(ready, 1)

            def value(t):
                steps = [(lambda s, c=c: h_t[s][:, c, P * t:P * t + P], lambda s, c=c: wvo_s[s][:, c, :]) for c in range(C)]
                product(bank[VAL[t]][:], steps).then_inc(v_ready, 1)

            def rows(i):
                pe.wait_ge(r_made, i + 1)
                pe.wait_ge(gl_made, i * PAIR + 1)
                for t in range(T):
                    last = nc.tensor.transpose(bank[ROWS][:, P * t:P * t + P], r_l[:, t:t + 1].to_broadcast([P, P]),
                                               ident[:, 0])
                last.then_inc(rows_ready, 1)

            def transpose_square(dst, rows_of, b):
                for m in range(J):
                    for j in range(J):
                        last = nc.tensor.transpose(dst[:, N * m + P * j:N * m + P * j + P],
                                                   rows_of[:, J * b + j, P * m:P * m + P], ident[:, 0])
                return last

            def transpose_k(i, banks=KT):
                for b in range(PAIR):
                    pe.wait_ge(k_made, i * T + J * b + J)
                    transpose_square(bank[banks[b]], k_nm, b).then_inc(kt_ready, 1)

            def aggregate(i):
                pe.wait_ge(v_split, i * T + T)
                for t in range(T):
                    b, j = t // J, t % J
                    pe.wait_ge(kt_split, i * PAIR + b + 1)
                    steps = [(lambda s, m=m: k_t[s][:, J * b + m, P * j:P * j + P], lambda s, m=m: v_s[s][:, J * b + m, :])
                             for m in range(J)]
                    product(bank[AGG[t]][:], steps).then_inc(agg_ready, 1)

            def body(i, mix_ahead, norm_ahead):
                prev = later(i)
                if norm_ahead:
                    pe.wait_ge(ht_split, i * C + C)
                    if not prev:
                        pe.wait_ge(weights_split, 1)
                    for e in range(C):
                        pe.wait_ge(mix_out, i * T + T + e + 1)
                        projection(ZL, e, wl_s, zl_ready)
                else:
                    last_lang()
                if not prev:
                    pe.wait_ge(weights_split, 2)
                for e in range(C):
                    projection(ZG, e, wg_s, zg_ready)
                pe.wait_ge(zl_split, i * C + C)
                gram(GRAM_L, zl_t, gram_l_ready)
                if prev:
                    transpose_k(i - 1)
                pe.wait_ge(zg_split, i * C + C)
                gram(GRAM_G, zg_t, gram_g_ready)
                if prev:
                    aggregate(i - 1)
                for b in range(PAIR):
                    pe.wait_ge(sl_out, i * PAIR + b + 1)
                    transpose_square(bank[SYM_L[b]], a_l, b).then_inc(sl_t_ready, 1)
                for t in range(T):
                    if t == (2 if norm_ahead else 0):
                        for b in range(PAIR):
                            pe.wait_ge(sg_out, i * T + J * b + J)
                            transpose_square(bank[SYM_G[b]], a_g, b).then_inc(sg_t_ready, 1)
                    if t == (2 if norm_ahead else 1):
                        rows(i)
                    if prev:
                        pe.wait_ge(y_sum, i * T - T + t + 1)
                    value(t)
                if norm_ahead:
                    pe.wait_ge(h_ready, i * T + 2 * T)
                    for c in range(C):
                        if c < 2:
                            pe.wait_ge(d2_made, i * PAIR + c + 1)
                        else:
                            pe.wait_ge(v_split, i * T + c - 1)
                        transpose_h(c)
                if mix_ahead:
                    pe.wait_ge(x_split, i + 2)
                    for t in range(T):
                        if t < 1:
                            pe.wait_ge(rows_out, i + 1)
                        elif t < 2:
                            pe.wait_ge(gl_made, i * PAIR + PAIR)
                        else:
                            pe.wait_ge(v_split, i * T + t + 1)
                        mix_begin(t)
                    with pe.If(mix_has_lo != 0):
                        mix_lo_passes()
                    mix_end()

            pe.wait_ge(mix_made, 4)
            for t in range(T):
                pe.wait_ge(first_split, t // J + 1)
                mix_begin(t)
            mix_lo_passes()
            mix_end()
            pe.wait_ge(mix_lo_known, 1)
            mix_has_lo = pe.value_load(mix_lo_max[0:1, 1:2].bitcast(mybir.dt.int32))
            pe.wait_ge(vo_loaded, 32)
            for c in range(C):
                for v in range(C):
                    last = nc.tensor.matmul(bank[HT[c]][:], wv_raw[:, v, P * c:P * c + P], wo_raw[:, v, :],
                                            start=(v == 0), stop=(v == C - 1))
                last.then_inc(wvo_ready, 1)
            pe.wait_ge(h_ready, T)
            for c in range(C):
                pe.wait_ge(wvo_split, c + 1)
                transpose_h(c)
            pe.wait_ge(x_split, 1)
            for t in range(T):
                pe.wait_ge(mix_out, t + 1)
                mix_begin(t)
            with pe.If(mix_has_lo != 0):
                mix_lo_passes()
            mix_end()
            body(0, True, True)
            body(1, True, True)
            with pe.Fori(2, G - 2) as i:
                body(i, True, True)
            body(G - 2, False, True)
            body(G - 1, False, False)
            transpose_k(G - 1, SYM_G)
            aggregate(G - 1)

    return nc


def kernel(x, adj, L0_gnn_bias, L1_gnn_W_lang, L1_gnn_W_grav, L1_gnn_W_V, L1_gnn_W_O, L1_gnn_gate_logit,
           L1_gnn_log_sigma):
    import numpy as np
    import concourse.bacc as bacc
    from concourse.bass_utils import run_bass_kernel_spmd

    arrays = {
        "x": np.ascontiguousarray(x),
        "adj": np.ascontiguousarray(adj),
        "bias": np.ascontiguousarray(L0_gnn_bias).reshape(1, -1),
        "w_lang_t": np.ascontiguousarray(np.asarray(L1_gnn_W_lang).T),
        "w_grav_t": np.ascontiguousarray(np.asarray(L1_gnn_W_grav).T),
        "w_v": np.ascontiguousarray(L1_gnn_W_V),
        "w_o_t": np.ascontiguousarray(np.asarray(L1_gnn_W_O).T),
        "gate": np.ascontiguousarray(L1_gnn_gate_logit).reshape(1, 1),
        "log_sigma": np.ascontiguousarray(L1_gnn_log_sigma).reshape(1, 1),
    }
    nc = bacc.Bacc("TRN2", target_bir_lowering=False, num_devices=1)
    args = [nc.dram_tensor(name, a.shape, F32, kind="ExternalInput").ap() for name, a in arrays.items()]
    out = nc.dram_tensor("out", arrays["x"].shape, F32, kind="ExternalOutput").ap()
    bass_adj_resnorm_kernel(nc, *args, out)
    return run_bass_kernel_spmd(nc, [arrays], core_ids=[0]).results[0]["out"]
```
